# Optimizing a Trainium2 kernel written in Bass

```python
import numpy as np
import jax
import jax.numpy as jnp

def _softmax(x, axis=-1):
    return jax.nn.softmax(x, axis=axis)

def _gelu(x):
    return jax.nn.gelu(x, approximate=True)

def _silu(x):
    return jax.nn.silu(x)

def _sigmoid(x):
    return jax.nn.sigmoid(x)

def _layernorm(x, axis=-1, eps=1e-05):
    m = jnp.mean(x, axis=axis, keepdims=True)
    v = jnp.var(x, axis=axis, keepdims=True)
    return (x - m) / jnp.sqrt(v + eps)

def _scatter_add(tgt, idx, src, axis=0):
    return tgt.at[idx].add(src)

def _segment_sum(src, seg, n):
    return jax.ops.segment_sum(src, seg, n)
kernel_name = 'mk_gnn_preln_d2_gnn_r16_5bac3f'

def setup_inputs(seed: int=0):
    np.random.seed(seed)
    _w = jnp.asarray

    def _rec_inputs():
        import jax
        import jax.numpy as jnp
        _gk = jax.random.key(seed)
        x = -0.0005121 + 1.001 * jax.random.normal(jax.random.fold_in(_gk, 1), (3125, 64), jnp.float32)
        _s = jax.random.randint(jax.random.fold_in(_gk, 2), (50000,), 0, 3125, jnp.int32)
        _d = jax.random.randint(jax.random.fold_in(_gk, 3), (50000,), 0, 3125, jnp.int32)
        _loop = jnp.arange(3125, dtype=jnp.int32)
        src = jnp.concatenate([_s, _d, _loop])
        dst = jnp.concatenate([_d, _s, _loop])
        _o = jnp.argsort(dst, stable=True)
        src = src[_o]
        dst = dst[_o]
        edge_attr_64 = 9.41057e-06 + 1 * jax.random.normal(jax.random.fold_in(_gk, 12), (103125, 64), jnp.float32)
        node_vec1 = jax.random.uniform(jax.random.fold_in(_gk, 14), (3125, 1), jnp.float32, 0.0, 0.999993)
        node_vec1_n2 = jax.random.uniform(jax.random.fold_in(_gk, 15), (3125, 1), jnp.float32, 0.0, 0.999993)
        return (x, src, dst, edge_attr_64, node_vec1, node_vec1_n2)
    x, src, dst, edge_attr_64, node_vec1, node_vec1_n2 = _rec_inputs()

    def _L0_gnn_setup():
        import jax, jax.numpy as jnp
        import numpy as np
        H = 5
        NEG_SLOPE = 0.2
        N_NODES = 3125
        N_EDGES = 25000
        IN_CH = 64
        OUT_CH = 64

        def gatv2_layer(x, src, dst, Wl, bl, Wr, br, att, bias, n_nodes):
            C = att.shape[1]
            xl = (x @ Wl + bl).reshape(n_nodes, H, C)
            xr = (x @ Wr + br).reshape(n_nodes, H, C)
            e = jax.nn.leaky_relu(xl[src] + xr[dst], NEG_SLOPE)
            alpha = jnp.einsum('ehc,hc->eh', e, att)
            m = jax.ops.segment_max(alpha, dst, num_segments=n_nodes)
            m = jnp.where(jnp.isfinite(m), m, 0.0)
            a = jnp.exp(alpha - m[dst])
            denom = jax.ops.segment_sum(a, dst, num_segments=n_nodes)
            a = a / (denom[dst] + 1e-16)
            out = jax.ops.segment_sum(a[:, :, None] * xl[src], dst, num_segments=n_nodes)
            return out.mean(axis=1) + bias
        key = jax.random.key(seed)
        ks = jax.random.split(key, 17)
        s = 0.05
        inp = {'x': jax.random.normal(ks[0], (N_NODES, IN_CH), jnp.float32), 'edge_index': jax.random.randint(ks[1], (2, N_EDGES), 0, N_NODES, jnp.int64), 'W1l': jax.random.normal(ks[2], (IN_CH, H * IN_CH), jnp.float32) * s, 'b1l': jnp.zeros((H * IN_CH,), jnp.float32), 'W1r': jax.random.normal(ks[3], (IN_CH, H * IN_CH), jnp.float32) * s, 'b1r': jnp.zeros((H * IN_CH,), jnp.float32), 'att1': jax.random.normal(ks[4], (H, IN_CH), jnp.float32) * s, 'bias1': jnp.zeros((IN_CH,), jnp.float32), 'W2l': jax.random.normal(ks[5], (IN_CH, H * OUT_CH), jnp.float32) * s, 'b2l': jnp.zeros((H * OUT_CH,), jnp.float32), 'W2r': jax.random.normal(ks[6], (IN_CH, H * OUT_CH), jnp.float32) * s, 'b2r': jnp.zeros((H * OUT_CH,), jnp.float32), 'att2': jax.random.normal(ks[7], (H, OUT_CH), jnp.float32) * s, 'bias2': jnp.zeros((OUT_CH,), jnp.float32), 'Wfc': jax.random.normal(ks[8], (OUT_CH, OUT_CH), jnp.float32) * s, 'bfc': jnp.zeros((OUT_CH,), jnp.float32)}
        return inp
    _L0_gnn_all = _L0_gnn_setup()
    _L0_gnn_in = {k: v for k, v in _L0_gnn_all.items() if k in ('W1l', 'b1l', 'W1r', 'b1r', 'att1', 'bias1', 'W2l', 'b2l', 'W2r', 'b2r', 'att2', 'bias2', 'Wfc', 'bfc')}
    del _L0_gnn_all

    def _L1_gnn_setup():
        import jax, jax.numpy as jnp
        import numpy as np
        N = 6250
        E = 200000
        D = 64
        key = jax.random.key(seed)
        k = jax.random.split(key, 7)
        weight = jax.random.normal(k[0], (N, D), dtype=jnp.float32) * 0.05
        ps_w = jax.random.normal(k[1], (1, D), dtype=jnp.float32) * 0.1
        review_feat = jax.random.normal(k[2], (E, D), dtype=jnp.float32)
        cj = jax.random.uniform(k[3], (N, 1), dtype=jnp.float32)
        ci = jax.random.uniform(k[4], (N, 1), dtype=jnp.float32)
        src = jax.random.randint(k[5], (E,), 0, N, dtype=jnp.int32)
        dst = jax.random.randint(k[6], (E,), 0, N, dtype=jnp.int32)
        return {'weight': weight, 'ps_w': ps_w, 'review_feat': review_feat, 'cj': cj, 'ci': ci, 'src': src, 'dst': dst}
    _L1_gnn_all = _L1_gnn_setup()
    _L1_gnn_in = {k: v for k, v in _L1_gnn_all.items() if k in ('ps_w',)}
    del _L1_gnn_all
    return {'x': x, 'src': src, 'dst': dst, 'edge_attr_64': edge_attr_64, 'node_vec1': node_vec1, 'node_vec1_n2': node_vec1_n2, 'L0_gnn_W1l': _L0_gnn_in['W1l'], 'L0_gnn_b1l': _L0_gnn_in['b1l'], 'L0_gnn_W1r': _L0_gnn_in['W1r'], 'L0_gnn_b1r': _L0_gnn_in['b1r'], 'L0_gnn_att1': _L0_gnn_in['att1'], 'L0_gnn_bias1': _L0_gnn_in['bias1'], 'L0_gnn_W2l': _L0_gnn_in['W2l'], 'L0_gnn_b2l': _L0_gnn_in['b2l'], 'L0_gnn_W2r': _L0_gnn_in['W2r'], 'L0_gnn_b2r': _L0_gnn_in['b2r'], 'L0_gnn_att2': _L0_gnn_in['att2'], 'L0_gnn_bias2': _L0_gnn_in['bias2'], 'L0_gnn_Wfc': _L0_gnn_in['Wfc'], 'L0_gnn_bfc': _L0_gnn_in['bfc'], 'L1_gnn_ps_w': _L1_gnn_in['ps_w']}

def reference(x, src, dst, edge_attr_64, node_vec1, node_vec1_n2, L0_gnn_W1l, L0_gnn_b1l, L0_gnn_W1r, L0_gnn_b1r, L0_gnn_att1, L0_gnn_bias1, L0_gnn_W2l, L0_gnn_b2l, L0_gnn_W2r, L0_gnn_b2r, L0_gnn_att2, L0_gnn_bias2, L0_gnn_Wfc, L0_gnn_bfc, L1_gnn_ps_w):
    import jax
    import jax.numpy as jnp

    def _L0_gnn_ref(x, edge_index, W1l, b1l, W1r, b1r, att1, bias1, W2l, b2l, W2r, b2r, att2, bias2, Wfc, bfc):
        import jax, jax.numpy as jnp
        import numpy as np
        H = 5
        NEG_SLOPE = 0.2
        N_NODES = 3125
        N_EDGES = 25000
        IN_CH = 64
        OUT_CH = 64

        def gatv2_layer(x, src, dst, Wl, bl, Wr, br, att, bias, n_nodes):
            C = att.shape[1]
            xl = (x @ Wl + bl).reshape(n_nodes, H, C)
            xr = (x @ Wr + br).reshape(n_nodes, H, C)
            e = jax.nn.leaky_relu(xl[src] + xr[dst], NEG_SLOPE)
            alpha = jnp.einsum('ehc,hc->eh', e, att)
            m = jax.ops.segment_max(alpha, dst, num_segments=n_nodes)
            m = jnp.where(jnp.isfinite(m), m, 0.0)
            a = jnp.exp(alpha - m[dst])
            denom = jax.ops.segment_sum(a, dst, num_segments=n_nodes)
            a = a / (denom[dst] + 1e-16)
            out = jax.ops.segment_sum(a[:, :, None] * xl[src], dst, num_segments=n_nodes)
            return out.mean(axis=1) + bias
        n = x.shape[0]
        loop = jnp.arange(n, dtype=edge_index.dtype)
        src = jnp.concatenate([edge_index[0], loop])
        dst = jnp.concatenate([edge_index[1], loop])
        h = jax.nn.relu(gatv2_layer(x, src, dst, W1l, b1l, W1r, b1r, att1, bias1, n))
        h = jax.nn.relu(gatv2_layer(h, src, dst, W2l, b2l, W2r, b2r, att2, bias2, n))
        return h @ Wfc + bfc

    def _L1_gnn_ref(weight, ps_w, review_feat, cj, ci, src, dst):
        import jax, jax.numpy as jnp
        import numpy as np
        N = 6250
        E = 200000
        D = 64
        feat = weight * cj
        pa = jax.nn.sigmoid(review_feat @ ps_w.T)
        msg = pa * feat[src]
        h = jax.ops.segment_sum(msg, dst, num_segments=weight.shape[0])
        return h * ci
    edge_index = jnp.stack([src, dst])
    h = jnp.maximum(_layernorm(x, axis=-1), 0.0)
    x = x + _L0_gnn_ref(h, edge_index, L0_gnn_W1l, L0_gnn_b1l, L0_gnn_W1r, L0_gnn_b1r, L0_gnn_att1, L0_gnn_bias1, L0_gnn_W2l, L0_gnn_b2l, L0_gnn_W2r, L0_gnn_b2r, L0_gnn_att2, L0_gnn_bias2, L0_gnn_Wfc, L0_gnn_bfc)
    h = jnp.maximum(_layernorm(x, axis=-1), 0.0)
    x = x + _L1_gnn_ref(h, L1_gnn_ps_w, edge_attr_64, node_vec1, node_vec1_n2, src, dst)
    return x

_drawn_inputs = setup_inputs


def setup_inputs(seed=0):
    import zlib

    import numpy as np

    out = dict(_drawn_inputs(seed))
    spreads = {'L0_gnn_b1l': (0.0, 0.8),
     'L0_gnn_b1r': (0.0, 2.0),
     'L0_gnn_bias1': (0.0, 0.8),
     'L0_gnn_b2l': (0.0, 0.575),
     'L0_gnn_b2r': (0.0, 2.0),
     'L0_gnn_bias2': (0.0, 0.493),
     'L0_gnn_bfc': (0.0, 0.1)}
    factors = {'L0_gnn_W1l': 8.0,
     'L0_gnn_W1r': 8.0,
     'L0_gnn_att1': 8.0,
     'L0_gnn_W2l': 8.0,
     'L0_gnn_W2r': 8.0,
     'L0_gnn_att2': 8.0}
    for name, (base, spread) in spreads.items():
        noise = np.random.default_rng([zlib.crc32(name.encode()), seed]).standard_normal(out[name].shape)
        drawn = base * np.exp(spread * noise) if base else spread * noise
        out[name] = jnp.asarray(drawn.astype(out[name].dtype))
    for name, factor in factors.items():
        out[name] = (out[name] * factor).astype(out[name].dtype)
    return out
```

```python
from contextlib import ExitStack

import numpy as np

import concourse.bass as bass
from concourse import mybir

P = 128
N = 3125
E = 103125
F = 64
H = 5
HF = H * F
WN = 25
W = N // WN
HW = H * WN
CN = 5 * WN
NC = N // CN
LIN = 2 * H
ZC = HF + LIN
ROW = ZC + F + 1
ROWP = ROW + 1
ZQ = [P, P, ZC - 2 * P]
T = -(-E // P)
TC = -(-T // P)
LAST = E - P
U = 4
ITER = U * U
NIT = -(-(T + W - 1) // ITER)
ITEMS = NIT * ITER
HALF = ITEMS // 2
IG = 8
IP = ITEMS // IG
RMAX = -(-(T * W) // ITEMS)
KX = 3 * WN
KO = KX + 1
BIG = 1.0e30
EPS = 1e-5

F32 = mybir.dt.float32
BF16 = mybir.dt.bfloat16
I32 = mybir.dt.int32
ALU = mybir.AluOpType
ACT = mybir.ActivationFunctionType
AX = mybir.AxisListType


def constant_columns():
    widths = [("ident", P), ("before", P), ("ones", P), ("headmask", 3 * HW), ("linsel", HW),
              ("outside", HW), ("nodesel", WN), ("winsel", 5), ("slot", 1), ("item_col", IG),
              ("tile_col", TC), ("item_row", ITEMS)]
    at, c = {}, 0
    for name, w in widths:
        at[name] = (c, w)
        c += w
    return at, c


def shape_constants():
    at, total = constant_columns()
    a = np.zeros((P, total), np.float32)
    p = np.arange(P)[:, None]

    def put(name, value):
        c, w = at[name]
        a[:, c:c + w] = value

    head = np.arange(HW)[None, :] // WN
    node = np.arange(HW)[None, :] % WN
    put("ident", p == np.arange(P)[None, :])
    put("before", p < np.arange(P)[None, :])
    put("ones", 1.0)
    put("headmask", np.concatenate([(q * P + p) // F == head for q in range(3)], axis=1))
    put("linsel", 1.0 * (p - F == head) - 1.0 * (p - F - H == head))
    put("outside", np.where((p < WN) & (p != node) | (p == KX), -BIG, 0.0))
    put("nodesel", (p % WN == np.arange(WN)[None, :]) & (p < CN))
    put("winsel", p // WN == np.arange(5)[None, :])
    put("slot", np.where(p < KX, p % WN, np.where(p == KX, WN, -7)))
    put("item_col", p + IP * np.arange(IG)[None, :])
    put("tile_col", p + P * np.arange(TC)[None, :])
    put("item_row", np.arange(ITEMS)[None, :])
    return a


def build_program(nc, x, src, dst, edge_attr, node_vec1, node_vec1_n2,
                  W1l, b1l, W1r, b1r, att1, bias1, W2l, b2l, W2r, b2r, att2, bias2,
                  Wfc, bfc, ps_w, consts, out):
    Wl, bl, Wr, br = [W1l, W2l], [b1l, b2l], [W1r, W2r], [b1r, b2r]
    att, gat_bias = [att1, att2], [bias1, bias2]
    at, ncols = constant_columns()
    ctx = ExitStack()

    def sb(name, shape, dt=F32):
        return ctx.enter_context(nc.sbuf_tensor(name, shape, dt))

    def sem(name):
        return ctx.enter_context(nc.semaphore(name))

    def dram(name, shape, dt=F32):
        return nc.dram_tensor(name, shape, dt).ap()

    with ctx:
        gat_rows = [dram(f"gat_rows{l}", [N, ROWP]) for l in range(2)]
        dst_rows = [dram(f"dst_rows{l}", [W + 1, KX, ZC], BF16) for l in range(2)]
        feat_rows = dram("feat_rows", [N, F])
        resid_rows = dram("resid_rows", [N, F])
        src_tab = dram("src_tab", [RMAX, P, ITEMS], I32)
        rel_tab = dram("rel_tab", [RMAX, P, ITEMS])
        relT_tab = dram("relT_tab", [RMAX, ITEMS, P], BF16)
        win_tab = dram("win_tab", [RMAX, ITEMS], I32)
        first_tab = dram("first_tab", [RMAX, ITEMS], I32)

        cst = sb("cst", [P, ncols])

        def const(name, rows=P):
            c, w = at[name]
            return cst[0:rows, c:c + w]

        outside = sb("outside", [P, HW], BF16)
        wl_ext = sb("wl_ext", [F + 1, 2, ROW])
        wr_ext = sb("wr_ext", [F + 1, 2, ZC])
        wfc_ext = sb("wfc_ext", [F + 1, F])
        att_row = sb("att_row", [P, 2, HF])
        att_col = sb("att_col", [P, 2, 3])
        att_mat = sb("att_mat", [P, 2, 3, HW])
        bias_tmp = sb("bias_tmp", [F + 1, HF])
        lin_tmp = sb("lin_tmp", [F + 1, HF])
        lin_sum = sb("lin_sum", [F + 1, H])
        bl_cols = sb("bl_cols", [F, 2, H])
        bias_col = sb("bias_col", [F, 2])
        out_bias = sb("out_bias", [F, 2])
        ps_row = sb("ps_row", [P, F])
        zero_rows = sb("zero_rows", [KX, ZC], BF16)

        early_a = sb("early_a", [P, (W + 1) * F])
        early_b = sb("early_b", [P, W * F])

        def part(n):
            return early_b[:, n * TC * P:(n + 1) * TC * P].rearrange("p (c e) -> p c e", c=TC)
        src_f, dst_y, win_base = part(0), part(1), part(2)
        src_i, dst_i = part(3).bitcast(I32), part(4).bitcast(I32)
        pick = early_a[:, 0:TC * ITEMS].rearrange("p (c i) -> p c i", c=TC)
        dst_f = sb("dst_f", [P, TC, P + 1])
        ext = sb("ext", [P, 2, TC])
        extw = sb("extw", [P, 2, TC])
        fl_i = sb("fl_i", [P, 2 * TC], I32)
        fl_f = sb("fl_f", [P, 2 * TC])
        fl_r = sb("fl_r", [P, 2 * TC])
        fl_a = sb("fl_a", [P, 2 * TC])
        cnt = sb("cnt", [P, TC])
        cum = sb("cum", [P, TC])
        first = sb("first", [P, TC])
        end = sb("end", [P, TC])
        rounds_f = sb("rounds_f", [P, 1])
        rounds_w = sb("rounds_w", [P, 1])
        rounds_i = sb("rounds_i", [P, 1], I32)
        acc_buf = sb("acc_buf", [P, (W + 1) * (F + 1)])

        def table(n, rows_=P):
            return acc_buf[0:rows_, n * ITEMS:(n + 1) * ITEMS]
        ge, src_o, rel_o, win_f = table(0), table(1).bitcast(I32), table(2), table(3)
        win_o, first_f, first_o = table(4, 1).bitcast(I32), table(5, 1), table(6, 1).bitcast(I32)
        relT_f = acc_buf[0:IP, 7 * ITEMS:7 * ITEMS + IG * P].rearrange("p (g e) -> p g e", g=IG)
        relT_m = early_b[0:IP, 5 * TC * P:5 * TC * P + IG * P].rearrange("p (g e) -> p g e", g=IG)
        win_c = sb("win_c", [IP, IG])
        relT_o = sb("relT_o", [IP, IG, P], BF16)

        xs = sb("xs", [CN, NC, F])
        xc_buf, xq_buf = sb("xc_buf", [P, NC * F]), sb("xq_buf", [P, NC * F])
        xc = xc_buf[0:CN, :].rearrange("p (c f) -> p c f", f=F)
        xq = xq_buf[0:CN, :].rearrange("p (c f) -> p c f", f=F)
        st = sb("st", [CN, 4, NC])
        cj = sb("cj", [CN, NC])
        ci = sb("ci", [WN, W])
        h_node = sb("h_node", [CN, F])
        h_T = sb("h_T", [F + 1, CN])
        row_o = sb("row_o", [CN, ROWP])
        parts = sb("parts", [CN, 3, ZC], BF16)
        rest = sb("rest", [CN, ZC])
        z_loop = sb("z_loop", [CN, HF])
        s_loop = sb("s_loop", [CN, 3, H])
        d_loop = sb("d_loop", [CN, H, WN])
        inv_l = sb("inv_l", [HW, 5])
        mean_x = sb("mean_x", [HW, 5, F])
        mean_T = sb("mean_T", [F, 5, HW])

        neg_max = sb("neg_max", [HW, W + 1])
        acc = acc_buf[0:HW, :].rearrange("p (w f) -> p w f", f=F + 1)
        acc2 = early_a[0:WN, :].rearrange("p (w f) -> p w f", f=F)
        resid = early_b[0:WN, :].rearrange("p (w f) -> p w f", f=F)

        src_s = xc_buf[:, 0:ITEMS].bitcast(I32)
        rel_s = xq_buf[:, 0:ITEMS]
        win_s = sb("win_s", [1, ITEMS], I32)
        first_s = sb("first_s", [1, ITEMS], I32)
        idx = sb("idx", [P, U, U], I32)
        rows = early_b[:, 0:U * U * ROWP].rearrange("p (s j k) -> p s j k", s=U, j=U)
        n_relu = 2 * 3 * U * P
        relu = early_a[:, 0:n_relu].rearrange("p (b z e) -> p b z e", b=2, z=3)
        dst_w = early_a[0:KO, n_relu:n_relu + U * U * ZC // 2].bitcast(BF16).rearrange(
            "p (s j k) -> p s j k", s=U, j=U)
        rel_b = sb("rel_b", [KO, U, U * P], BF16)
        oh = sb("oh", [KO, 2, U * P], BF16)
        p_T = sb("p_T", [HW, 2, U, P])
        p_e = sb("p_e", [P, U, HW])
        neg_item = sb("neg_item", [HW, 2, U])
        nm = sb("nm", [HW, 2, U])
        dm = sb("dm", [HW, 2, U])
        scale = sb("scale", [HW, 2, U])
        feat_g = sb("feat_g", [P, U, U, F])
        ea = sb("ea", [P, U, U, F])
        pre = sb("pre", [P, 2, U])
        pa = sb("pa", [P, 2, U])
        oh2 = sb("oh2", [P, U, WN])
        gate = sb("gate", [P, 2, U, WN])

        ps = ctx.enter_context(nc.psum_tensor("ps", [P, 8, 512], F32))

        loaded, phase = sem("loaded"), sem("phase")
        zeroed, weights_done = sem("zeroed"), sem("weights_done")
        counted, prefix_done, picked = sem("counted"), sem("prefix_done"), sem("picked")
        expanded, moved, expandedT, tab_ready, tab_stored = (
            sem("expanded"), sem("moved"), sem("expandedT"), sem("tab_ready"), sem("tab_stored"))
        var_done, sd_done = sem("var_done"), sem("sd_done")
        zero_stored = sem("zero_stored")
        node_names = ["h_node_done", "h_turned", "h_T_done", "proj_done", "row_done", "parts_done",
                      "loop_spread", "loop_turned", "loop_done", "stored",
                      "mean_done", "mean_turned", "mean_T_done", "mixed", "fc_done", "resid_done"]
        node_sem = [{n: sem(f"{n}{g}") for n in node_names} for g in range(3)]
        node_dma = [sem(f"node_dma{l}") for l in range(2)]
        acc_init, tab_loaded = sem("acc_init"), [sem(f"tab_loaded{g}") for g in range(3)]
        edge_names = ["idx_done", "oh_done", "z_done0", "z_done1", "z_done2", "relu_done0",
                      "relu_done1", "relu_done2", "logit_done0", "logit_done1", "max_done0",
                      "max_done1", "state_done0", "state_done1", "state_done2", "state_done3",
                      "nm_done0", "nm_done1", "p_done", "scale_done", "p_turned", "p_e_done",
                      "sum_done", "acc_done0", "acc_done1", "acc_done2", "acc_done3"]
        es = {n: sem(n) for n in edge_names}
        gate_names = ["idx2_done", "prod_done", "pre_done", "pa_done", "oh2_done", "gate_done",
                      "sum2_done", "acc2_done0", "acc2_done1", "acc2_done2", "acc2_done3"]
        gs = {n: sem(n) for n in gate_names}
        gathered = [sem(f"gathered{u}") for u in range(U)]
        rel_loaded = [sem(f"rel_loaded{u}") for u in range(U)]
        dst_loaded = [sem(f"dst_loaded{u}") for u in range(U)]
        gathered2 = [sem(f"gathered2_{u}") for u in range(U)]
        ea_loaded = [sem(f"ea_loaded{u}") for u in range(U)]
        held_sp, held_pool, held_pe = sem("held_sp"), sem("held_pool"), sem("held_pe")
        final_done, feat_done, out_stored = sem("final_done"), sem("feat_done"), sem("out_stored")
        feat_stored, resid_loaded = sem("feat_stored"), sem("resid_loaded")

        n_loads = [0]
        held = {}

        def n_rounds(eng):
            return eng.value_load(rounds_i[0:1, 0:1], min_val=1, max_val=RMAX)

        def hold(eng, semaphore, value):
            eng.wait_ge(semaphore, value)
            eng.sem_inc(held[eng], 1)

        def barrier(eng, n):
            eng.drain().then_inc(phase, 1)
            eng.wait_ge(phase, 5 * n)

        def window_regs(eng, engine_type, table, col, top):
            _, regs = nc.values_load_multi_w_load_instructions(
                table[0:1, bass.ds(col, U)], engines=[engine_type], min_val=0, max_val=top)
            return regs

        def edge_rounds(eng, layer, per_round, body):
            R = n_rounds(eng)
            with eng.Fori(0, R) as r:
                k_round = eng.snap((r + layer * R) * (U * NIT) + U)
                per_round(r, k_round)
                body(0, k_round, True, False)
                with eng.Fori(1, NIT - 1) as q:
                    body(q, eng.snap(k_round + q * U), False, False)
                body(NIT - 1, eng.snap(k_round + (NIT - 1) * U), False, True)

        block = ctx.enter_context(nc.Block())

        @block.sync
        def _(sp):
            held[sp] = held_sp
            def load(dst_ap, src_ap):
                n_loads[0] += 16
                with nc.allow_non_contiguous_dma(reason="small weights and columns"):
                    sp.dma_start(dst_ap, src_ap).then_inc(loaded, 16)

            sp.wait_ge(zeroed, 1)
            full = (TC - 1) * P * P
            rest_tiles = T - 1 - (TC - 1) * P
            for buf, arr in ((dst_i, dst), (src_i, src)):
                load(buf[:, 0:TC - 1, :], arr[0:full].rearrange("(c p e) -> p c e", c=TC - 1, p=P))
                load(buf[0:rest_tiles, TC - 1, :],
                     arr[full:full + rest_tiles * P].rearrange("(p e) -> p e", p=rest_tiles))
                seen = (T - 1) * P - LAST
                load(buf[rest_tiles:rest_tiles + 1, TC - 1, seen:P],
                     arr[(T - 1) * P:E].rearrange("(a e) -> a e", a=1))
            load(cst[:, :], consts)
            load(xs[:, :, :], x.rearrange("(c p) f -> p c f", p=CN))
            for l in range(2):
                load(wl_ext[0:F, l, 0:HF], Wl[l])
                load(wr_ext[0:F, l, 0:HF], Wr[l])
                load(wr_ext[F:F + 1, l, 0:HF], bl[l].rearrange("(a k) -> a k", a=1))
                load(att_row[:, l, :], att[l].rearrange("h f -> (h f)").partition_broadcast(P))
                flat = att[l].rearrange("h f -> (h f)")
                for q in range(3):
                    n = min(P, HF - q * P)
                    load(att_col[0:n, l, q:q + 1], flat[q * P:q * P + n].rearrange("(p a) -> p a", a=1))
                load(bl_cols[:, l, :], bl[l].rearrange("(h f) -> f h", f=F))
                load(bias_col[:, l:l + 1], gat_bias[l].rearrange("(p a) -> p a", a=1))
            load(wfc_ext[0:F, :], Wfc)
            load(wfc_ext[F:F + 1, :], bfc.rearrange("(a k) -> a k", a=1))
            load(ps_row[:, :], ps_w.rearrange("a f -> (a f)").partition_broadcast(P))
            load(cj[:, :], node_vec1.rearrange("(c p) a -> p (c a)", p=CN))
            load(ci[:, :], node_vec1_n2.rearrange("(w n) a -> n (w a)", n=WN))
            load(lin_tmp[F:F + 1, :], br[0].rearrange("(a k) -> a k", a=1))
            load(bias_tmp[F:F + 1, :], br[1].rearrange("(a k) -> a k", a=1))
            for l in range(2):
                sp.dma_start(dst_rows[l][W], zero_rows[:, :]).then_inc(zero_stored, 16)
            sp.wait_ge(zero_stored, 32)

            sp.wait_ge(counted, 2)
            R = n_rounds(sp)
            with sp.Fori(0, R) as r:
                hold(sp, tab_ready, r + 1)
                one = bass.ds(r, 1)
                sp.dma_start(src_tab[one].rearrange("a p i -> (a p) i"), src_o[:, :]).then_inc(tab_stored, 16)
                sp.dma_start(rel_tab[one].rearrange("a p i -> (a p) i"), rel_o[:, :]).then_inc(tab_stored, 16)
                sp.dma_start(win_tab[one], win_o[:, :]).then_inc(tab_stored, 16)
                sp.dma_start(first_tab[one], first_o[:, :]).then_inc(tab_stored, 16)
                sp.dma_start(relT_tab[one].rearrange("a (g p) e -> (a p) g e", p=IP),
                             relT_o[:, :, :]).then_inc(tab_stored, 16)
                hold(sp, tab_stored, (r + 1) * 80)
            barrier(sp, 1)

            def store_projections(l, c):
                ns = node_sem[l]
                hold(sp, ns["row_done"], c + 2)
                sp.dma_start(gat_rows[l][bass.ds(c * CN, CN), :], row_o[:, :]).then_inc(node_dma[l], 16)
                hold(sp, ns["parts_done"], c + 2)
                for v in range(5):
                    sp.dma_start(
                        dst_rows[l][bass.ds(c * 5 + v, 1)].rearrange("a (s n) z -> (a n) s z", n=WN),
                        parts[v * WN:(v + 1) * WN, :, :]).then_inc(node_dma[l], 16)
                hold(sp, node_dma[l], (c + 1) * 96)
                sp.sem_inc(ns["stored"], 1)

            def start_state(l):
                for h in range(H):
                    sp.dma_start(acc[h * WN:(h + 1) * WN, 0:W, :],
                                 gat_rows[l].rearrange("(w n) k -> n w k", n=WN)[:, :, ZC:ROW]
                                 ).then_inc(acc_init, 16)
                sp.wait_ge(acc_init, 16 * H * (l + 1))

            def load_table(g, r, bufs):
                one = bass.ds(r, 1)
                for buf, tab in bufs:
                    ap = tab[one]
                    sp.dma_start(buf[:, :], ap.rearrange("a p i -> (a p) i") if len(ap.shape) == 3 else ap
                                 ).then_inc(tab_loaded[g], 16)
                hold(sp, tab_loaded[g], (r + 1) * (16 * len(bufs)))

            def edges(l):
                def per_round(r, k):
                    hold(sp, es["acc_done3"], k)
                    load_table(l, r, ((src_s, src_tab), (win_s, win_tab)))
                    cur[0] = r

                def body(q, k, is_first, is_last):
                    for u in range(U):
                        col = q * ITER + u * U
                        wins = window_regs(sp, mybir.EngineType.SP, win_s, col, W)
                        hold(sp, es["oh_done"], k + (u - 3))
                        sp.dma_start(rel_b[:, u, :],
                                     relT_tab[bass.ds(cur[0], 1), bass.ds(col, U), :].rearrange(
                                         "a i e -> (a i e)").partition_broadcast(KO)
                                     ).then_inc(rel_loaded[u], 16)
                        hold(sp, es["z_done2"], k + (u - 3))
                        for j in range(U):
                            sp.dma_start(dst_w[0:KX, u, j, :],
                                         dst_rows[l][bass.ds(wins[j], 1)].rearrange("a k z -> (a k) z")
                                         ).then_inc(dst_loaded[u], 16)
                cur = [0]
                edge_rounds(sp, l, per_round, body)

            for l in range(2):
                with sp.Fori(0, NC) as c:
                    store_projections(l, c)
                barrier(sp, 2 + 3 * l)
                start_state(l)
                barrier(sp, 3 + 3 * l)
                edges(l)
                barrier(sp, 4 + 3 * l)
            sp.wait_ge(feat_done, 1)
            sp.dma_start(feat_rows.rearrange("(c p) f -> p c f", p=CN), xq[:, :, :]).then_inc(feat_stored, 16)
            sp.dma_start(resid_rows.rearrange("(c p) f -> p c f", p=CN), xs[:, :, :]).then_inc(feat_stored, 16)
            sp.wait_ge(feat_stored, 32)
            sp.dma_start(resid[:, :, :], resid_rows.rearrange("(w n) f -> n w f", n=WN)).then_inc(resid_loaded, 16)
            barrier(sp, 8)

            def per_round2(r, k):
                hold(sp, gs["acc2_done3"], k)
                load_table(2, r, ((src_s, src_tab), (rel_s, rel_tab), (win_s, win_tab), (first_s, first_tab)))

            def body2(q, k, is_first, is_last):
                for u in range(U):
                    col = q * ITER + u * U
                    firsts = window_regs(sp, mybir.EngineType.SP, first_s, col, LAST)
                    hold(sp, gs["pre_done"], k + (u - 3))
                    for j in range(U):
                        sp.dma_start(ea[:, u, j, :], edge_attr[bass.ds(firsts[j], P), :]
                                     ).then_inc(ea_loaded[u], 16)
            edge_rounds(sp, 0, per_round2, body2)
            sp.wait_ge(final_done, 1)
            sp.dma_start(out.rearrange("(w n) f -> n w f", n=WN), acc2[:, 0:W, :]).then_inc(out_stored, 16)
            sp.wait_ge(out_stored, 16)

        @block.gpsimd
        def _(pool):
            held[pool] = held_pool
            for s in list(es.values()) + list(gs.values()):
                pool.sem_inc(s, U)
            for ns in node_sem:
                for s in ns.values():
                    pool.sem_inc(s, 1)
            pool.wait_ge(counted, 2)
            barrier(pool, 1)

            def gathers(target, table, width, sems, done, used):
                def body(q, k, is_first, is_last):
                    for u in range(U):
                        pool.wait_ge(used, k + (u - 3))
                        hold(pool, done, k + (u + 1))
                        for j in range(U):
                            pool.indirect_dma_start(
                                out=target[:, u, j, :], out_offset=None, in_=table,
                                in_offset=bass.IndirectOffsetOnAxis(ap=idx[:, u, j:j + 1], axis=0)
                            ).then_inc(sems[u], 16)
                return body
            for l in range(2):
                barrier(pool, 2 + 3 * l)
                barrier(pool, 3 + 3 * l)
                edge_rounds(pool, l, lambda r, k: None,
                            gathers(rows, gat_rows[l][:, :], ROWP, gathered, es["idx_done"], es["sum_done"]))
                barrier(pool, 4 + 3 * l)
            barrier(pool, 8)
            edge_rounds(pool, 0, lambda r, k: None,
                        gathers(feat_g, feat_rows[:, :], F, gathered2, gs["idx2_done"], gs["sum2_done"]))

        @block.scalar
        def _(act):
            def root(n):
                act.wait_ge(var_done, n)
                act.activation(st[:, 2, :], st[:, 1, :], ACT.Sqrt).then_inc(sd_done, 1)

            act.wait_ge(counted, 2)
            barrier(act, 1)
            root(1)

            def project(l, c):
                ns = node_sem[l]
                act.wait_ge(ns["proj_done"], c + 2)
                act.wait_ge(ns["stored"], c + 1)
                act.wait_ge(ns["loop_done"], c + 1)
                act.activation(row_o[:, 0:ROW], ps[0:CN, 0, 0:ROW], ACT.Copy).then_inc(ns["row_done"], 1)

            def turn_mean(ns, c):
                act.wait_ge(ns["mean_turned"], c + 2)
                act.wait_ge(ns["mixed"], c + 1)
                act.activation(mean_T[:, 0:4, :].rearrange("p v k -> p (v k)"), ps[0:F, 4, 0:4 * HW], ACT.Copy)
                act.activation(mean_T[:, 4, :], ps[0:F, 5, 0:HW], ACT.Copy).then_inc(ns["mean_T_done"], 1)

            def mix(ns, l, c, used):
                act.wait_ge(ns["mixed"], c + 2)
                act.wait_ge(used, c + 1)
                act.activation(h_T[0:F, :], ps[0:F, 6, 0:CN], ACT.Relu, bias=out_bias[:, l:l + 1],
                               scale=1.0 / H).then_inc(ns["h_T_done"], 1)

            def edges(l):
                def make_idx(q, k, u, table_col):
                    act.wait_ge(es["sum_done"], k + (u - 3))
                    act.copy(idx[:, u % U, :], src_s[:, bass.ds(table_col, U)]).then_inc(es["idx_done"], 1)

                def per_round(r, k):
                    act.wait_ge(tab_loaded[l], (r + 1) * 32)
                    for u in range(2):
                        make_idx(0, k, u, u * U)

                def exps(k, u):
                    b = u % 2
                    act.wait_ge(es["p_turned"], k + (u - 1))
                    for j in range(U):
                        if j % 2 == 0:
                            act.wait_ge(es[f"nm_done{j // 2}"], k + (u + 1))
                        i = act.activation(p_T[:, b, j, :], ps[0:HW, 3 + j // 2, (j % 2) * P:(j % 2 + 1) * P], ACT.Exp,
                                           bias=nm[:, b, j:j + 1])
                    i.then_inc(es["p_done"], 1)
                    act.wait_ge(es["acc_done3"], k + (u - 1))
                    act.activation(scale[:, b, :], dm[:, b, :], ACT.Exp).then_inc(es["scale_done"], 1)

                def body(q, k, is_first, is_last):
                    for u in range(U):
                        b = u % 2
                        act.wait_ge(es["logit_done1"], k + (u - 1))
                        for z in range(2):
                            act.wait_ge(es[f"z_done{z}"], k + (u + 1))
                            act.activation(relu[:, b, z, :], ps[:, z, :], ACT.Relu
                                           ).then_inc(es[f"relu_done{z}"], 1)
                        if not (is_first and u == 0):
                            exps(k, u - 1)
                        if not (is_last and u >= 2):
                            make_idx(q, k, u + 2, q * ITER + (u + 2) * U)
                    if is_last:
                        exps(k, U - 1)
                edge_rounds(act, l, per_round, body)

            ns = node_sem[0]
            with act.Fori(0, NC) as c:
                act.wait_ge(ns["h_turned"], c + 2)
                act.wait_ge(ns["proj_done"], c + 1)
                act.activation(h_T[0:F, :], ps[0:F, 2, 0:CN], ACT.Copy).then_inc(ns["h_T_done"], 1)
                project(0, c)
            barrier(act, 2)
            barrier(act, 3)
            edges(0)
            barrier(act, 4)
            ns = node_sem[1]
            with act.Fori(0, NC) as c:
                turn_mean(ns, c)
                mix(ns, 0, c, ns["proj_done"])
                project(1, c)
            barrier(act, 5)
            barrier(act, 6)
            edges(1)
            barrier(act, 7)
            ns = node_sem[2]
            with act.Fori(0, NC) as c:
                turn_mean(ns, c)
                mix(ns, 1, c, ns["fc_done"])
            root(2)
            barrier(act, 8)

            def make_idx2(k, u, table_col):
                act.wait_ge(gs["sum2_done"], k + (u - 3))
                act.copy(idx[:, u % U, :], src_s[:, bass.ds(table_col, U)]).then_inc(gs["idx2_done"], 1)

            def per_round2(r, k):
                act.wait_ge(tab_loaded[2], (r + 1) * 64)
                for u in range(2):
                    make_idx2(k, u, u * U)

            def body2(q, k, is_first, is_last):
                for u in range(U):
                    act.wait_ge(gs["pre_done"], k + (u + 1))
                    act.wait_ge(gs["gate_done"], k + (u - 1))
                    act.activation(pa[:, u % 2, :], pre[:, u % 2, :], ACT.Sigmoid).then_inc(gs["pa_done"], 1)
                    if not (is_last and u >= 2):
                        make_idx2(k, u + 2, q * ITER + (u + 2) * U)
            edge_rounds(act, 0, per_round2, body2)

        @block.tensor
        def _(pe):
            held[pe] = held_pe
            mm = pe.matmul
            ident = const("ident")

            def turn(o, i, rows_, start=True, stop=True):
                return mm(o, i, cst[0:rows_, at["ident"][0]:at["ident"][0] + rows_], start=start, stop=stop,
                          is_transpose=True)

            pe.wait_ge(counted, 1)
            mm(ps[:, 0, 0:TC], const("before"), cnt[:, :], start=True, stop=False)
            mm(ps[:, 0, 0:TC], const("ones"), fl_f[:, 0:TC], start=False, stop=True)
            mm(ps[:, 1, 0:1], const("ones"), cum[:, TC - 1:TC], start=True, stop=True).then_inc(prefix_done, 1)
            pe.wait_ge(counted, 2)
            R = n_rounds(pe)
            with pe.Fori(0, R) as r:
                for t in range(TC):
                    pe.wait_ge(picked, r * TC + (t + 1))
                    for a, lhs in enumerate((src_f[:, t, :], dst_f[:, t, 0:P], win_base[:, t, :],
                                             cst[:, at["tile_col"][0] + t:at["tile_col"][0] + t + 1])):
                        for hh in range(2):
                            m = mm(ps[0:P if a < 3 else 1, 2 * a + hh, 0:HALF], lhs,
                                   pick[:, t, hh * HALF:(hh + 1) * HALF], start=(t == 0), stop=(t == TC - 1))
                m.then_inc(expanded, 1)
                pe.wait_ge(moved, r + 1)
                for g in range(IG):
                    for t in range(TC):
                        m = mm(ps[0:IP, g // 3, (g % 3) * (P + 1):(g % 3 + 1) * (P + 1)],
                               pick[:, t, g * IP:(g + 1) * IP], dst_f[:, t, :], start=(t == 0), stop=(t == TC - 1))
                m.then_inc(expandedT, 1)
            barrier(pe, 1)

            def project(l, c):
                ns = node_sem[l]
                pe.wait_ge(ns["h_T_done"], c + 2)
                pe.wait_ge(ns["row_done"], c + 1)
                pe.wait_ge(ns["loop_spread"], c + 1)
                mm(ps[0:CN, 0, 0:ROW], h_T[:, :], wl_ext[:, l, :], start=True, stop=True)
                mm(ps[0:CN, 1, 0:ZC], h_T[:, :], wr_ext[:, l, :], start=True, stop=True
                   ).then_inc(ns["proj_done"], 1)

            def spread_loops(l, c):
                ns = node_sem[l]
                pe.wait_ge(ns["loop_spread"], c + 2)
                pe.wait_ge(ns["loop_done"], c + 1)
                mm(ps[0:HW, 3, 0:5], d_loop[:, :, :].rearrange("p h n -> p (h n)"), const("winsel", CN),
                   start=True, stop=True).then_inc(ns["loop_turned"], 1)

            def turn_mean(ns, c):
                pe.wait_ge(ns["mean_done"], c + 2)
                hold(pe, ns["mean_T_done"], c + 1)
                for v in range(5):
                    m = turn(ps[0:F, 4 + v // 4, (v % 4) * HW:(v % 4 + 1) * HW], mean_x[:, v, :], HW)
                m.then_inc(ns["mean_turned"], 1)

            def mix(ns, l, c):
                pe.wait_ge(ns["mean_T_done"], c + 2)
                hold(pe, ns["h_T_done"], c + 1)
                for h in range(H):
                    m = mm(ps[0:F, 6, 0:CN], wl_ext[0:F, l, h * F:(h + 1) * F],
                           mean_T[:, :, h * WN:(h + 1) * WN], start=(h == 0), stop=(h == H - 1))
                m.then_inc(ns["mixed"], 1)

            def edges(l):
                def z_step(k, u):
                    b = u % 2
                    pe.wait_ge(gathered[u], k * 16)
                    pe.wait_ge(dst_loaded[u], k * 16)
                    pe.wait_ge(es["oh_done"], k + (u + 1))
                    for z in range(3):
                        n = ZQ[z]
                        pe.wait_ge(es[f"relu_done{z}"], k + u)
                        for j in range(U):
                            o = ps[0:n, z, j * P:(j + 1) * P]
                            turn(o, rows[:, u, j, z * P:z * P + n], P, stop=False)
                            m = mm(o, dst_w[:, u, j, z * P:z * P + n], oh[:, b, j * P:(j + 1) * P],
                                   start=False, stop=True)
                        m.then_inc(es[f"z_done{z}"], 1)

                def logits(k, u):
                    b = u % 2
                    for z in range(3):
                        pe.wait_ge(es[f"relu_done{z}"], k + (u + 1))
                    pe.wait_ge(es["p_done"], k + u)
                    for hh in range(2):
                        cols = slice(hh * 2 * P, (hh + 1) * 2 * P)
                        o = ps[0:HW, 3 + hh, 0:2 * P]
                        mm(o, outside[0:KO, :], oh[:, b, cols], start=True, stop=False)
                        for z in range(3):
                            n = ZQ[z]
                            m = mm(o, att_mat[0:n, l, z, :], relu[0:n, b, z, cols], start=False, stop=(z == 2))
                        m.then_inc(es[f"logit_done{hh}"], 1)

                def turn_p(k, u):
                    pe.wait_ge(es["p_done"], k + (u + 1))
                    pe.wait_ge(es["p_e_done"], k + u)
                    for j in range(U):
                        m = turn(ps[:, 5, j * HW:(j + 1) * HW], p_T[:, u % 2, j, :], HW)
                    m.then_inc(es["p_turned"], 1)

                def sums(k, u):
                    pe.wait_ge(es["p_e_done"], k + (u + 1))
                    pe.wait_ge(es["acc_done3"], k + u)
                    for j in range(U):
                        m = mm(ps[0:HW, 6, j * (F + 1):(j + 1) * (F + 1)], p_e[:, j, :],
                               rows[:, u % U, j, ZC:ROW], start=True, stop=True)
                    m.then_inc(es["sum_done"], 1)

                def body(q, k, is_first, is_last):
                    for u in range(U):
                        z_step(k, u)
                        if not (is_first and u < 2):
                            turn_p(k, u - 2)
                        if not (is_first and u < 1):
                            logits(k, u - 1)
                        if not (is_first and u < 2):
                            sums(k, u - 2)
                    if is_last:
                        turn_p(k, U - 2)
                        logits(k, U - 1)
                        sums(k, U - 2)
                        turn_p(k, U - 1)
                        sums(k, U - 1)
                edge_rounds(pe, l, lambda r, k: None, body)

            ns = node_sem[0]
            with pe.Fori(0, NC) as c:
                pe.wait_ge(ns["h_node_done"], c + 2)
                hold(pe, ns["h_T_done"], c + 1)
                turn(ps[0:F, 2, 0:CN], h_node[:, :], CN).then_inc(ns["h_turned"], 1)
                project(0, c)
                spread_loops(0, c)
            barrier(pe, 2)
            barrier(pe, 3)
            edges(0)
            barrier(pe, 4)
            ns = node_sem[1]
            with pe.Fori(0, NC) as c:
                turn_mean(ns, c)
                mix(ns, 0, c)
                project(1, c)
                spread_loops(1, c)
            barrier(pe, 5)
            barrier(pe, 6)
            edges(1)
            barrier(pe, 7)
            ns = node_sem[2]
            with pe.Fori(0, NC) as c:
                turn_mean(ns, c)
                mix(ns, 1, c)
                pe.wait_ge(ns["h_T_done"], c + 2)
                pe.wait_ge(ns["resid_done"], c + 1)
                mm(ps[0:CN, 7, 0:F], h_T[:, :], wfc_ext[:, :], start=True, stop=True).then_inc(ns["fc_done"], 1)
            barrier(pe, 8)

            def body2(q, k, is_first, is_last):
                for u in range(U):
                    b = u % 2
                    pe.wait_ge(gathered2[u], k * 16)
                    pe.wait_ge(gs["gate_done"], k + (u + 1))
                    pe.wait_ge(gs["acc2_done3"], k + (u - 1))
                    for j in range(U):
                        m = mm(ps[0:WN, b, j * F:(j + 1) * F], gate[:, b, j, :], feat_g[:, u, j, :],
                               start=True, stop=True)
                    m.then_inc(gs["sum2_done"], 1)
            edge_rounds(pe, 0, lambda r, k: None, body2)

        @block.vector
        def _(dve):
            TT, TS, STT, CP = dve.tensor_tensor, dve.tensor_scalar, dve.scalar_tensor_tensor, dve.tensor_copy

            def settle():
                dve.drain()

            dve.memset(src_i[:, TC - 1, :], 0)
            dve.memset(dst_i[:, TC - 1, :], -1)
            dve.memset(zero_rows[:, :], 0.0)
            dve.memset(wl_ext[:, :, :], 0.0)
            dve.memset(att_col[:, :, :], 0.0)
            dve.memset(h_T[:, :], 1.0)
            dve.memset(row_o[:, :], 0.0)
            dve.memset(neg_max[:, :], 0.0)
            settle()
            dve.memset(cum[:, :], 1.0).then_inc(zeroed, 1)
            dve.wait_ge(loaded, n_loads[0])

            CP(dst_f[:, :, 0:P], dst_i[:, :, :])
            CP(src_f[:, :, :], src_i[:, :, :])
            settle()
            TS(dst_y[:, :, :], dst_f[:, :, 0:P], 0.0, 1.0e6, ALU.is_lt, ALU.mult)
            dve.tensor_reduce(ext[:, 1, :], dst_f[:, :, 0:P], AX.X, ALU.max)
            settle()
            TT(dst_y[:, :, :], dst_y[:, :, :], dst_f[:, :, 0:P], ALU.add)
            settle()
            dve.tensor_reduce(ext[:, 0, :], dst_y[:, :, :], AX.X, ALU.min)
            settle()

            def floor_div(o, a, d, n):
                TS(fl_i[:, 0:n], a, 1.0 / d, None, ALU.mult)
                settle()
                CP(fl_f[:, 0:n], fl_i[:, 0:n])
                settle()
                STT(fl_r[:, 0:n], fl_f[:, 0:n], -float(d), a, ALU.mult, ALU.add)
                settle()
                TS(fl_a[:, 0:n], fl_r[:, 0:n], float(d), None, ALU.is_ge)
                TS(fl_r[:, 0:n], fl_r[:, 0:n], 0.0, None, ALU.is_lt)
                settle()
                TT(fl_a[:, 0:n], fl_a[:, 0:n], fl_r[:, 0:n], ALU.subtract)
                settle()
                TT(o, fl_a[:, 0:n], fl_f[:, 0:n], ALU.add)
                settle()

            floor_div(extw[:, :, :].rearrange("p a c -> p (a c)"), ext[:, :, :].rearrange("p a c -> p (a c)"),
                      WN, 2 * TC)
            TT(cnt[:, :], extw[:, 1, :], extw[:, 0, :], ALU.subtract)
            settle()
            TS(cnt[:, :], cnt[:, :], 1.0, 0.0, ALU.add, ALU.max)
            settle()
            dve.tensor_tensor_scan(cum[:, :], cst[:, at["ones"][0]:at["ones"][0] + TC], cnt[:, :], 0.0,
                                   ALU.mult, ALU.add)
            settle()
            TT(fl_f[:, 0:TC], cum[:, :], cnt[:, :], ALU.subtract)
            settle()
            dve.memset(fl_r[:, :], 0.0).then_inc(counted, 1)
            dve.wait_ge(prefix_done, 1)
            CP(first[:, :], ps[:, 0, 0:TC])
            TS(rounds_f[:, :], ps[:, 1, 0:1], float(ITEMS - 1), None, ALU.add)
            settle()
            TT(end[:, :], first[:, :], cnt[:, :], ALU.add)
            TT(dst_f[:, :, P], extw[:, 0, :], first[:, :], ALU.subtract)
            floor_div(rounds_w[:, :], rounds_f[:, :], ITEMS, 1)
            CP(rounds_i[:, :], rounds_w[:, :])
            settle()
            dve.memset(fl_r[:, :], 0.0).then_inc(counted, 1)

            R = n_rounds(dve)
            with dve.Fori(0, R) as r:
                CP(win_base[:, :, :], dst_f[:, :, P:P + 1].to_broadcast([P, TC, P]))
                settle()
                for t in range(TC):
                    TS(ge[:, :], const("item_row"), first[:, t:t + 1], None, ALU.is_ge)
                    settle()
                    STT(pick[:, t, :], const("item_row"), end[:, t:t + 1], ge[:, :], ALU.is_lt, ALU.mult
                        ).then_inc(picked, 1)
                    settle()
                dve.wait_ge(expanded, r + 1)

                def halves(a, n=P):
                    return ps[0:n, 2 * a:2 * a + 2, 0:HALF]

                def two(ap):
                    return ap.rearrange("p (a b) -> p a b", a=2)
                CP(two(src_o[:, :]), halves(0))
                TT(two(win_f[:, :]), halves(2), two(const("item_row")), ALU.add)
                TS(two(first_f[:, :]), halves(3, 1), float(P), float(LAST), ALU.mult, ALU.min)
                settle()
                TS(win_f[:, :], win_f[:, :], float(W), None, ALU.min)
                settle()
                STT(two(rel_o[:, :]), two(win_f[:, :]), -float(WN), halves(1), ALU.mult, ALU.add)
                CP(win_o[:, :], win_f[0:1, :])
                CP(first_o[:, :], first_f[:, :])
                settle()
                dve.memset(fl_r[:, :], 0.0).then_inc(moved, 1)
                dve.wait_ge(expandedT, r + 1)
                for g in range(IG):
                    o = ps[0:IP, g // 3, (g % 3) * (P + 1):(g % 3 + 1) * (P + 1)]
                    TT(win_c[:, g:g + 1], o[:, P:P + 1], const("item_col", IP)[:, g:g + 1], ALU.add)
                settle()
                TS(win_c[:, :], win_c[:, :], float(W), -float(WN), ALU.min, ALU.mult)
                settle()
                for g in range(IG):
                    o = ps[0:IP, g // 3, (g % 3) * (P + 1):(g % 3 + 1) * (P + 1)]
                    TS(relT_f[:, g, :], o[:, 0:P], win_c[:, g:g + 1], None, ALU.add)
                settle()
                TS(relT_m[:, :, :], relT_f[:, :, :], 0.0, None, ALU.is_ge)
                settle()
                STT(relT_m[:, :, :], relT_f[:, :, :], float(WN - 1), relT_m[:, :, :], ALU.is_le, ALU.mult)
                settle()
                STT(relT_f[:, :, :], relT_f[:, :, :], float(WN), relT_m[:, :, :], ALU.subtract, ALU.mult)
                settle()
                TS(relT_o[:, :, :], relT_f[:, :, :], float(WN), None, ALU.add)
                TS(first[:, :], first[:, :], -float(ITEMS), None, ALU.add)
                TS(end[:, :], end[:, :], -float(ITEMS), None, ALU.add)
                TS(dst_f[:, :, P], dst_f[:, :, P], float(ITEMS), None, ALU.add)
                settle()
                dve.memset(fl_r[:, :], 0.0).then_inc(tab_ready, 1)
                dve.wait_ge(tab_stored, (r + 1) * 80)

            CP(outside[:, :], const("outside"))
            TT(wr_ext[F:F + 1, 0, 0:HF], wr_ext[F:F + 1, 0, 0:HF], lin_tmp[F:F + 1, :], ALU.add)
            TT(wr_ext[F:F + 1, 1, 0:HF], wr_ext[F:F + 1, 1, 0:HF], bias_tmp[F:F + 1, :], ALU.add)
            for l in range(2):
                CP(wl_ext[:, l, ZC:ROW], cst[0:F + 1, at["ident"][0]:at["ident"][0] + F + 1])
                dve.tensor_reduce(out_bias[:, l:l + 1], bl_cols[:, l, :], AX.X, ALU.add)
                for z in range(3):
                    TS(att_mat[:, l, z, :], cst[:, at["headmask"][0] + z * HW:at["headmask"][0] + (z + 1) * HW],
                       att_col[:, l, z:z + 1], 0.8, ALU.mult, ALU.mult)
            settle()
            for l in range(2):
                TT(att_mat[:, l, 2, :], att_mat[:, l, 2, :], const("linsel"), ALU.add)
                STT(out_bias[:, l:l + 1], out_bias[:, l:l + 1], 1.0 / H, bias_col[:, l:l + 1], ALU.mult, ALU.add)
                for w_ext in (wl_ext, wr_ext):
                    TT(lin_tmp[:, :], w_ext[:, l, 0:HF], att_row[0:F + 1, l, :], ALU.mult)
                    settle()
                    dve.tensor_reduce(lin_sum[:, :], lin_tmp[:, :].rearrange("p (h f) -> p h f", h=H), AX.X, ALU.add)
                    settle()
                    TS(w_ext[:, l, HF:HF + H], lin_sum[:, :], 0.2, None, ALU.mult)
                    TS(w_ext[:, l, HF + H:ZC], lin_sum[:, :], -0.2, None, ALU.mult)
                    settle()
            barrier(dve, 1)
            dve.memset(dst_w[:, :, :, :], 0.0)
            dve.memset(acc[:, :, :], 1.0)

            def center(n):
                dve.tensor_reduce(st[:, 0, :], xs[:, :, :], AX.X, ALU.add)
                settle()
                TS(st[:, 0, :], st[:, 0, :], 1.0 / F, None, ALU.mult)
                settle()
                TT(xc[:, :, :], xs[:, :, :], st[:, 0, :].unsqueeze(2).to_broadcast([CN, NC, F]), ALU.subtract)
                settle()
                TT(xq[:, :, :], xc[:, :, :], xc[:, :, :], ALU.mult)
                settle()
                dve.tensor_reduce(st[:, 0, :], xq[:, :, :], AX.X, ALU.add)
                settle()
                TS(st[:, 1, :], st[:, 0, :], 1.0 / F, EPS, ALU.mult, ALU.add).then_inc(var_done, 1)
                dve.wait_ge(sd_done, n)
                dve.reciprocal(st[:, 3, :], st[:, 2, :])
                settle()

            def project(l, c):
                ns = node_sem[l]
                r_ps = ps[0:CN, 1, :]
                dve.wait_ge(ns["proj_done"], c + 2)
                dve.wait_ge(ns["stored"], c + 1)
                CP(parts[:, 0, :], r_ps[:, 0:ZC])
                settle()
                TT(rest[:, :], r_ps[:, 0:ZC], parts[:, 0, :], ALU.subtract)
                settle()
                CP(parts[:, 1, :], rest[:, :])
                settle()
                TT(parts[:, 2, :], rest[:, :], parts[:, 1, :], ALU.subtract).then_inc(ns["parts_done"], 1)
                dve.wait_ge(ns["row_done"], c + 2)
                TT(z_loop[:, :], row_o[:, 0:HF], r_ps[:, 0:HF], ALU.add)
                TT(s_loop[:, 0, :], row_o[:, HF:HF + H], r_ps[:, HF:HF + H], ALU.add)
                settle()
                STT(z_loop[:, :], z_loop[:, :], 0.0, att_row[0:CN, l, :], ALU.max, ALU.mult)
                settle()
                dve.tensor_reduce(s_loop[:, 1, :], z_loop[:, :].rearrange("p (h f) -> p h f", h=H), AX.X, ALU.add)
                settle()
                STT(s_loop[:, 2, :], s_loop[:, 1, :], 0.8, s_loop[:, 0, :], ALU.mult, ALU.add)
                settle()
                dve.wait_ge(ns["loop_turned"], c + 1)
                TT(d_loop[:, :, :], s_loop[:, 2, :].unsqueeze(2).to_broadcast([CN, H, WN]),
                   const("nodesel", CN).unsqueeze(1).to_broadcast([CN, H, WN]), ALU.mult
                   ).then_inc(ns["loop_spread"], 1)
                dve.wait_ge(ns["loop_turned"], c + 2)
                TS(neg_max[:, bass.ds(c * 5, 5)], ps[0:HW, 3, 0:5], -1.0, None, ALU.mult
                   ).then_inc(ns["loop_done"], 1)

            def mean(ns, c):
                dve.reciprocal(inv_l[:, :], acc[:, bass.ds(c * 5, 5), F])
                settle()
                dve.wait_ge(ns["mean_turned"], c + 1)
                TT(mean_x[:, :, :], acc[:, bass.ds(c * 5, 5), 0:F],
                   inv_l[:, :].unsqueeze(2).to_broadcast([HW, 5, F]), ALU.mult).then_inc(ns["mean_done"], 1)

            def edges(l):
                def one_hot(k, u):
                    dve.wait_ge(rel_loaded[u % U], (k + (4 * (u // U))) * 4)
                    dve.wait_ge(es["logit_done1"], k + (u - 1))
                    TS(oh[:, u % 2, :], rel_b[:, u % U, :], const("slot", KO), None, ALU.is_equal
                       ).then_inc(es["oh_done"], 1)

                def relu_last(k, u):
                    n = ZQ[2]
                    dve.wait_ge(es["logit_done1"], k + (u - 1))
                    dve.wait_ge(es["z_done2"], k + (u + 1))
                    TS(relu[0:n, u % 2, 2, :], ps[0:n, 2, :], 0.0, None, ALU.max).then_inc(es["relu_done2"], 1)

                def copy_p(k, u):
                    dve.wait_ge(es["p_turned"], k + (u + 1))
                    dve.wait_ge(es["sum_done"], k + u)
                    CP(p_e[:, :, :].rearrange("p j k -> p (j k)"), ps[:, 5, 0:U * HW]).then_inc(es["p_e_done"], 1)

                def maxima(k, u, col):
                    b = u % 2
                    wins = window_regs(dve, mybir.EngineType.DVE, win_s, col, W)
                    dve.wait_ge(es["scale_done"], k + (u - 1))
                    for hh in range(2):
                        dve.wait_ge(es[f"logit_done{hh}"], k + (u + 1))
                        dve.tensor_reduce(neg_item[:, b, 2 * hh:2 * hh + 2],
                                          ps[0:HW, 3 + hh, 0:2 * P].rearrange(
                                              "p (j e) -> p j e", j=2), AX.X, ALU.max, negate=True
                                          ).then_inc(es[f"max_done{hh}"], 1)
                        dve.wait_ge(es[f"max_done{hh}"], k + (u + 1))
                        for j in (2 * hh, 2 * hh + 1):
                            m = neg_item[:, b, j:j + 1]
                            state = neg_max[:, bass.ds(wins[j], 1)]
                            dve.wait_ge(es[f"state_done{(j - 1) % U}"], k + (u if j == 0 else u + 1))
                            TT(nm[:, b, j:j + 1], m, state, ALU.min)
                            i = TS(dm[:, b, j:j + 1], m, state, 0.0, ALU.subtract, ALU.min)
                            if j % 2:
                                i.then_inc(es[f"nm_done{hh}"], 1)
                            TT(state, m, state, ALU.min).then_inc(es[f"state_done{j}"], 1)

                def take_sums(k, u, col):
                    wins = window_regs(dve, mybir.EngineType.DVE, win_s, col, W)
                    dve.wait_ge(es["sum_done"], k + (u + 1))
                    dve.wait_ge(es["scale_done"], k + (u + 1))
                    for j in range(U):
                        a = acc[:, bass.ds(wins[j], 1), :].rearrange("p a f -> p (a f)")
                        dve.wait_ge(es[f"acc_done{(j - 1) % U}"], k + (u if j == 0 else u + 1))
                        STT(a, a, scale[:, u % 2, j:j + 1], ps[0:HW, 6, j * (F + 1):(j + 1) * (F + 1)],
                            ALU.mult, ALU.add).then_inc(es[f"acc_done{j}"], 1)

                def per_round(r, k):
                    dve.wait_ge(tab_loaded[l], (r + 1) * 32)
                    one_hot(k, 0)

                def body(q, k, is_first, is_last):
                    col = q * ITER
                    for u in range(U):
                        relu_last(k, u)
                        if not (is_first and u < 2):
                            copy_p(k, u - 2)
                        if not (is_first and u < 1):
                            maxima(k, u - 1, col + (u - 1) * U)
                        if not (is_last and u == U - 1):
                            one_hot(k, u + 1)
                        if not (is_first and u < 2):
                            take_sums(k, u - 2, col + (u - 2) * U)
                    if is_last:
                        copy_p(k, U - 2)
                        maxima(k, U - 1, col + (U - 1) * U)
                        take_sums(k, U - 2, col + (U - 2) * U)
                        copy_p(k, U - 1)
                        take_sums(k, U - 1, col + (U - 1) * U)
                edge_rounds(dve, l, per_round, body)

            center(1)
            ns = node_sem[0]
            with dve.Fori(0, NC) as c:
                dve.wait_ge(ns["h_turned"], c + 1)
                TS(h_node[:, :], xc[:, bass.ds(c, 1), :].rearrange("p a f -> p (a f)"),
                   st[:, 3, bass.ds(c, 1)], 0.0, ALU.mult, ALU.max).then_inc(ns["h_node_done"], 1)
                project(0, c)
            barrier(dve, 2)
            barrier(dve, 3)
            edges(0)
            barrier(dve, 4)
            ns = node_sem[1]
            with dve.Fori(0, NC) as c:
                mean(ns, c)
                project(1, c)
            barrier(dve, 5)
            barrier(dve, 6)
            edges(1)
            barrier(dve, 7)
            ns = node_sem[2]
            with dve.Fori(0, NC) as c:
                mean(ns, c)
                dve.wait_ge(ns["fc_done"], c + 2)
                xr = xs[:, bass.ds(c, 1), :].rearrange("p a f -> p (a f)")
                TT(xr, xr, ps[0:CN, 7, 0:F], ALU.add).then_inc(ns["resid_done"], 1)
            dve.memset(acc2[:, :, :], 0.0)
            settle()
            center(2)
            TT(xq[:, :, :], xc[:, :, :], st[:, 3, :].unsqueeze(2).to_broadcast([CN, NC, F]), ALU.mult)
            settle()
            TS(xq[:, :, :], xq[:, :, :], 0.0, None, ALU.max)
            settle()
            TT(xq[:, :, :], xq[:, :, :], cj[:, :].unsqueeze(2).to_broadcast([CN, NC, F]), ALU.mult
               ).then_inc(feat_done, 1)
            barrier(dve, 8)

            def product(k, u):
                dve.wait_ge(ea_loaded[u % U], (k + (4 * (u // U))) * 16)
                dve.wait_ge(gs["pa_done"], k + (u - 1))
                e = ea[:, u % U, :, :]
                TT(e, e, ps_row[:, :].unsqueeze(1).to_broadcast([P, U, F]), ALU.mult).then_inc(gs["prod_done"], 1)
                dve.wait_ge(gs["prod_done"], k + (u + 1))
                dve.tensor_reduce(pre[:, u % 2, :], e, AX.X, ALU.add).then_inc(gs["pre_done"], 1)

            def gates(k, u, col):
                TT(oh2[:, :, :], rel_s[:, bass.ds(col, U)].unsqueeze(2).to_broadcast([P, U, WN]),
                   cst[:, at["item_row"][0]:at["item_row"][0] + WN].unsqueeze(1).to_broadcast([P, U, WN]),
                   ALU.is_equal).then_inc(gs["oh2_done"], 1)
                dve.wait_ge(gs["oh2_done"], k + (u + 1))
                dve.wait_ge(gs["pa_done"], k + (u + 1))
                dve.wait_ge(gs["sum2_done"], k + (u - 1))
                TT(gate[:, u % 2, :, :], oh2[:, :, :], pa[:, u % 2, :].unsqueeze(2).to_broadcast([P, U, WN]),
                   ALU.mult).then_inc(gs["gate_done"], 1)

            def take_sums2(k, u, col):
                wins = window_regs(dve, mybir.EngineType.DVE, win_s, col, W)
                dve.wait_ge(gs["sum2_done"], k + (u + 1))
                for j in range(U):
                    a = acc2[:, bass.ds(wins[j], 1), :].rearrange("p a f -> p (a f)")
                    dve.wait_ge(gs[f"acc2_done{(j - 1) % U}"], k + (u if j == 0 else u + 1))
                    TT(a, a, ps[0:WN, u % 2, j * F:(j + 1) * F], ALU.add).then_inc(gs[f"acc2_done{j}"], 1)

            def per_round2(r, k):
                dve.wait_ge(tab_loaded[2], (r + 1) * 64)
                product(k, 0)

            def body2(q, k, is_first, is_last):
                for u in range(U):
                    if not (is_last and u == U - 1):
                        product(k, u + 1)
                    gates(k, u, q * ITER + u * U)
                    if not (is_first and u == 0):
                        take_sums2(k, u - 1, q * ITER + (u - 1) * U)
                if is_last:
                    take_sums2(k, U - 1, q * ITER + (U - 1) * U)
            edge_rounds(dve, 0, per_round2, body2)
            settle()
            dve.wait_ge(resid_loaded, 16)
            TT(acc2[:, 0:W, :], acc2[:, 0:W, :], ci[:, :].unsqueeze(2).to_broadcast([WN, W, F]), ALU.mult)
            settle()
            TT(acc2[:, 0:W, :], acc2[:, 0:W, :], resid[:, :, :], ALU.add).then_inc(final_done, 1)


INPUTS = ["x", "src", "dst", "edge_attr_64", "node_vec1", "node_vec1_n2",
          "L0_gnn_W1l", "L0_gnn_b1l", "L0_gnn_W1r", "L0_gnn_b1r", "L0_gnn_att1", "L0_gnn_bias1",
          "L0_gnn_W2l", "L0_gnn_b2l", "L0_gnn_W2r", "L0_gnn_b2r", "L0_gnn_att2", "L0_gnn_bias2",
          "L0_gnn_Wfc", "L0_gnn_bfc", "L1_gnn_ps_w"]


def kernel(**inputs):
    import concourse.bacc as bacc
    from concourse.bass_utils import run_bass_kernel_spmd

    nc = bacc.Bacc("TRN2", target_bir_lowering=False, num_devices=1)
    arrays, args = {}, []
    for name in INPUTS + ["constants"]:
        a = shape_constants() if name == "constants" else np.ascontiguousarray(inputs[name])
        arrays[f"in_{name}"] = a
        args.append(nc.dram_tensor(f"in_{name}", a.shape, mybir.dt.from_np(a.dtype), kind="ExternalInput").ap())
    out = nc.dram_tensor("out_0", (N, F), F32, kind="ExternalOutput").ap()
    build_program(nc, *args, out)
    result = run_bass_kernel_spmd(nc, [arrays], core_ids=[0])
    return result.results[0]["out_0"]
```

```python
from contextlib import ExitStack

import numpy as np

import concourse.bass as bass
from concourse import mybir

P = 128
N = 3125
E = 103125
F = 64
H = 5
HF = H * F
WN = 25
W = N // WN
HW = H * WN
CN = 5 * WN
NC = N // CN
LIN = 2 * H
ZC = HF + LIN
ROW = ZC + F + 1
ROWP = ROW + 1
ZQ = [P, P, ZC - 2 * P]
T = -(-E // P)
TC = -(-T // P)
LAST = E - P
U = 4
S = 6
AHEAD = 4
ITER = U * S
NIT = -(-(T + W - 1) // ITER)
ITEMS = NIT * ITER
HALF = ITEMS // 2
IG = 8
IP = ITEMS // IG
RMAX = -(-(T * W) // ITEMS)
KX = 3 * WN
KO = KX + 1
BIG = 1.0e30
EPS = 1e-5

F32 = mybir.dt.float32
BF16 = mybir.dt.bfloat16
I32 = mybir.dt.int32
ALU = mybir.AluOpType
ACT = mybir.ActivationFunctionType
AX = mybir.AxisListType


def constant_columns():
    widths = [("ident", P), ("before", P), ("ones", P), ("headmask", 3 * HW), ("linsel", HW),
              ("outside", HW), ("nodesel", WN), ("winsel", 5), ("slot", 1), ("item_col", IG),
              ("tile_col", TC), ("item_row", ITEMS)]
    at, c = {}, 0
    for name, w in widths:
        at[name] = (c, w)
        c += w
    return at, c


def shape_constants():
    at, total = constant_columns()
    a = np.zeros((P, total), np.float32)
    p = np.arange(P)[:, None]

    def put(name, value):
        c, w = at[name]
        a[:, c:c + w] = value

    head = np.arange(HW)[None, :] // WN
    node = np.arange(HW)[None, :] % WN
    put("ident", p == np.arange(P)[None, :])
    put("before", p < np.arange(P)[None, :])
    put("ones", 1.0)
    put("headmask", np.concatenate([(q * P + p) // F == head for q in range(3)], axis=1))
    put("linsel", 1.0 * (p - F == head) - 1.0 * (p - F - H == head))
    put("outside", np.where((p < WN) & (p != node) | (p == KX), -BIG, 0.0))
    put("nodesel", (p % WN == np.arange(WN)[None, :]) & (p < CN))
    put("winsel", p // WN == np.arange(5)[None, :])
    put("slot", np.where(p < KX, p % WN, np.where(p == KX, WN, -7)))
    put("item_col", p + IP * np.arange(IG)[None, :])
    put("tile_col", p + P * np.arange(TC)[None, :])
    put("item_row", np.arange(ITEMS)[None, :])
    return a


def build_program(nc, x, src, dst, edge_attr, node_vec1, node_vec1_n2,
                  W1l, b1l, W1r, b1r, att1, bias1, W2l, b2l, W2r, b2r, att2, bias2,
                  Wfc, bfc, ps_w, consts, out):
    Wl, bl, Wr, br = [W1l, W2l], [b1l, b2l], [W1r, W2r], [b1r, b2r]
    att, gat_bias = [att1, att2], [bias1, bias2]
    at, ncols = constant_columns()
    ctx = ExitStack()

    def sb(name, shape, dt=F32):
        return ctx.enter_context(nc.sbuf_tensor(name, shape, dt))

    def sem(name):
        return ctx.enter_context(nc.semaphore(name))

    def dram(name, shape, dt=F32):
        return nc.dram_tensor(name, shape, dt).ap()

    with ctx:
        gat_rows = [dram(f"gat_rows{l}", [N, ROWP]) for l in range(2)]
        dst_rows = [dram(f"dst_rows{l}", [W + 1, KX, ZC], BF16) for l in range(2)]
        feat_rows = dram("feat_rows", [N, F])
        resid_rows = dram("resid_rows", [N, F])
        src_tab = dram("src_tab", [RMAX, P, ITEMS], I32)
        rel_tab = dram("rel_tab", [RMAX, P, ITEMS])
        relT_tab = dram("relT_tab", [RMAX, ITEMS, P], BF16)
        win_tab = dram("win_tab", [RMAX, ITEMS], I32)
        first_tab = dram("first_tab", [RMAX, ITEMS], I32)

        cst = sb("cst", [P, ncols])

        def const(name, rows=P):
            c, w = at[name]
            return cst[0:rows, c:c + w]

        outside = sb("outside", [P, HW], BF16)
        wl_ext = sb("wl_ext", [F + 1, 2, ROW])
        wr_ext = sb("wr_ext", [F + 1, 2, ZC])
        wfc_ext = sb("wfc_ext", [F + 1, F])
        att_row = sb("att_row", [P, 2, HF])
        att_col = sb("att_col", [P, 2, 3])
        att_mat = sb("att_mat", [P, 2, 3, HW])
        bias_tmp = sb("bias_tmp", [F + 1, HF])
        lin_tmp = sb("lin_tmp", [F + 1, HF])
        lin_sum = sb("lin_sum", [F + 1, H])
        bl_cols = sb("bl_cols", [F, 2, H])
        bias_col = sb("bias_col", [F, 2])
        out_bias = sb("out_bias", [F, 2])
        ps_row = sb("ps_row", [P, F])
        zero_rows = sb("zero_rows", [KX, ZC], BF16)

        early_a = sb("early_a", [P, (W + 1) * F])
        early_b = sb("early_b", [P, S * U * ROWP])

        def part(n):
            return early_b[:, n * TC * P:(n + 1) * TC * P].rearrange("p (c e) -> p c e", c=TC)
        src_f, dst_y, win_base = part(0), part(1), part(2)
        src_i, dst_i = part(3).bitcast(I32), part(4).bitcast(I32)
        pick = early_a[:, 0:TC * ITEMS].rearrange("p (c i) -> p c i", c=TC)
        dst_f = sb("dst_f", [P, TC, P + 1])
        ext = sb("ext", [P, 2, TC])
        extw = sb("extw", [P, 2, TC])
        fl_i = sb("fl_i", [P, 2 * TC], I32)
        fl_f = sb("fl_f", [P, 2 * TC])
        fl_r = sb("fl_r", [P, 2 * TC])
        fl_a = sb("fl_a", [P, 2 * TC])
        cnt = sb("cnt", [P, TC])
        cum = sb("cum", [P, TC])
        first = sb("first", [P, TC])
        end = sb("end", [P, TC])
        rounds_f = sb("rounds_f", [P, 1])
        rounds_w = sb("rounds_w", [P, 1])
        rounds_i = sb("rounds_i", [P, 1], I32)
        acc_buf = sb("acc_buf", [P, (W + 1) * (F + 1)])

        def table(n, rows_=P):
            return acc_buf[0:rows_, n * ITEMS:(n + 1) * ITEMS]
        ge, src_o, rel_o, win_f = table(0), table(1).bitcast(I32), table(2), table(3)
        win_o, first_f, first_o = table(4, 1).bitcast(I32), table(5, 1), table(6, 1).bitcast(I32)
        relT_f = acc_buf[0:IP, 7 * ITEMS:7 * ITEMS + IG * P].rearrange("p (g e) -> p g e", g=IG)
        relT_m = early_b[0:IP, 5 * TC * P:5 * TC * P + IG * P].rearrange("p (g e) -> p g e", g=IG)
        win_c = sb("win_c", [IP, IG])
        relT_o = sb("relT_o", [IP, IG, P], BF16)

        xs = sb("xs", [CN, NC, F])
        xc_buf, xq_buf = sb("xc_buf", [P, NC * F]), sb("xq_buf", [P, NC * F])
        xc = xc_buf[0:CN, :].rearrange("p (c f) -> p c f", f=F)
        xq = xq_buf[0:CN, :].rearrange("p (c f) -> p c f", f=F)
        st = sb("st", [CN, 4, NC])
        cj = sb("cj", [CN, NC])
        ci = sb("ci", [WN, W])
        h_node = sb("h_node", [CN, F])
        h_T = sb("h_T", [F + 1, CN])
        row_o = sb("row_o", [CN, ROWP])
        parts = sb("parts", [CN, 3, ZC], BF16)
        rest = sb("rest", [CN, ZC])
        z_loop = sb("z_loop", [CN, HF])
        s_loop = sb("s_loop", [CN, 3, H])
        d_loop = sb("d_loop", [CN, H, WN])
        inv_l = sb("inv_l", [HW, 5])
        mean_x = sb("mean_x", [HW, 5, F])
        mean_T = sb("mean_T", [F, 5, HW])

        neg_max = sb("neg_max", [HW, W + 1])
        acc = acc_buf[0:HW, :].rearrange("p (w f) -> p w f", f=F + 1)
        acc2 = early_a[0:WN, :].rearrange("p (w f) -> p w f", f=F)
        resid = early_b[0:WN, 0:W * F].rearrange("p (w f) -> p w f", f=F)

        src_s = xc_buf[:, 0:ITEMS].bitcast(I32)
        rel_s = xq_buf[:, 0:ITEMS]
        win_s = sb("win_s", [1, ITEMS], I32)
        first_s = sb("first_s", [1, ITEMS], I32)
        idx = sb("idx", [P, S, U], I32)
        rows = early_b[:, :].rearrange("p (s j k) -> p s j k", s=S, j=U)
        n_relu = 2 * 3 * U * P
        relu = early_a[:, 0:n_relu].rearrange("p (b z e) -> p b z e", b=2, z=3)
        dst_w = early_a[0:KO, n_relu:n_relu + S * U * ZC // 2].bitcast(BF16).rearrange(
            "p (s j k) -> p s j k", s=S, j=U)
        rel_b = sb("rel_b", [KO, S, U * P], BF16)
        oh = sb("oh", [KO, 3, U * P], BF16)
        p_T = sb("p_T", [HW, 2, U, P])
        p_e = sb("p_e", [P, U, HW])
        neg_item = sb("neg_item", [HW, 2, U])
        nm = sb("nm", [HW, 2, U])
        dm = sb("dm", [HW, 2, U])
        scale = sb("scale", [HW, 2, U])
        feat_g = sb("feat_g", [P, S, U, F])
        ea = sb("ea", [P, S, U, F])
        pre = sb("pre", [P, 2, U])
        pa = sb("pa", [P, 2, U])
        oh2 = sb("oh2", [P, U, WN])
        gate = sb("gate", [P, 2, U, WN])

        ps = ctx.enter_context(nc.psum_tensor("ps", [P, 8, 512], F32))

        loaded, phase = sem("loaded"), sem("phase")
        zeroed, weights_done = sem("zeroed"), sem("weights_done")
        counted, prefix_done, picked = sem("counted"), sem("prefix_done"), sem("picked")
        expanded, moved, expandedT, tab_ready, tab_stored = (
            sem("expanded"), sem("moved"), sem("expandedT"), sem("tab_ready"), sem("tab_stored"))
        var_done, sd_done = sem("var_done"), sem("sd_done")
        zero_stored = sem("zero_stored")
        node_names = ["h_node_done", "h_turned", "h_T_done", "proj_done", "row_done", "parts_done",
                      "loop_spread", "loop_turned", "loop_done", "stored",
                      "mean_done", "mean_turned", "mean_T_done", "mixed", "fc_done", "resid_done"]
        node_sem = [{n: sem(f"{n}{g}") for n in node_names} for g in range(3)]
        node_dma = [sem(f"node_dma{l}") for l in range(2)]
        acc_init, tab_loaded = sem("acc_init"), [sem(f"tab_loaded{g}") for g in range(3)]
        edge_names = ["idx_done", "oh_done", "z_done0", "z_done1", "z_done2", "relu_done0",
                      "relu_done1", "relu_done2", "logit_done0", "logit_done1", "max_done0",
                      "max_done1", "state_done0", "state_done1", "state_done2", "state_done3",
                      "nm_done0", "nm_done1", "p_half_done", "p_done", "scale_done", "p_turned", "p_e_done",
                      "sum_done", "acc_done0", "acc_done1", "acc_done2", "acc_done3"]
        es = {n: sem(n) for n in edge_names}
        gate_names = ["idx2_done", "prod_done", "pre_done", "pa_done", "oh2_done", "gate_done",
                      "sum2_done", "acc2_done0", "acc2_done1", "acc2_done2", "acc2_done3"]
        gs = {n: sem(n) for n in gate_names}
        gathered = [sem(f"gathered{u}") for u in range(S)]
        rel_loaded = [sem(f"rel_loaded{u}") for u in range(S)]
        dst_loaded = [sem(f"dst_loaded{u}") for u in range(S)]
        gathered2 = [sem(f"gathered2_{u}") for u in range(S)]
        ea_loaded = [sem(f"ea_loaded{u}") for u in range(S)]
        held_sp, held_pool, held_pe = sem("held_sp"), sem("held_pool"), sem("held_pe")
        final_done, feat_done, out_stored = sem("final_done"), sem("feat_done"), sem("out_stored")
        feat_stored, resid_loaded = sem("feat_stored"), sem("resid_loaded")

        n_loads = [0]
        held = {}

        def n_rounds(eng):
            return eng.value_load(rounds_i[0:1, 0:1], min_val=1, max_val=RMAX)

        def hold(eng, semaphore, value):
            eng.wait_ge(semaphore, value)
            eng.sem_inc(held[eng], 1)

        def barrier(eng, n):
            eng.drain().then_inc(phase, 1)
            eng.wait_ge(phase, 5 * n)

        def logit_bank(u, hh):
            return (3, 4, 7)[(2 * u + hh) % 3]

        def window_regs(eng, engine_type, table, col, top):
            _, regs = nc.values_load_multi_w_load_instructions(
                table[0:1, bass.ds(col, U)], engines=[engine_type], min_val=0, max_val=top,
                skip_runtime_bounds_check_because="phase 1 clamps the tables to these bounds")
            return regs

        def edge_rounds(eng, layer, per_round, body):
            R = n_rounds(eng)
            with eng.Fori(0, R) as r:
                m_round = eng.snap((r + layer * R) * NIT + 1)
                per_round(r, eng.snap(m_round * S))

                def at_body(q):
                    m = eng.snap(m_round + q)
                    return q, eng.snap(m * S), m
                body(*at_body(0), True, False)
                with eng.Fori(1, NIT - 1) as q:
                    body(*at_body(q), False, False)
                body(*at_body(NIT - 1), False, True)

        block = ctx.enter_context(nc.Block())

        @block.sync
        def _(sp):
            held[sp] = held_sp
            def load(dst_ap, src_ap):
                n_loads[0] += 16
                with nc.allow_non_contiguous_dma(reason="small weights and columns"):
                    sp.dma_start(dst_ap, src_ap).then_inc(loaded, 16)

            sp.wait_ge(zeroed, 1)
            full = (TC - 1) * P * P
            rest_tiles = T - 1 - (TC - 1) * P
            for buf, arr in ((dst_i, dst), (src_i, src)):
                load(buf[:, 0:TC - 1, :], arr[0:full].rearrange("(c p e) -> p c e", c=TC - 1, p=P))
                load(buf[0:rest_tiles, TC - 1, :],
                     arr[full:full + rest_tiles * P].rearrange("(p e) -> p e", p=rest_tiles))
                seen = (T - 1) * P - LAST
                load(buf[rest_tiles:rest_tiles + 1, TC - 1, seen:P],
                     arr[(T - 1) * P:E].rearrange("(a e) -> a e", a=1))
            load(cst[:, :], consts)
            load(xs[:, :, :], x.rearrange("(c p) f -> p c f", p=CN))
            for l in range(2):
                load(wl_ext[0:F, l, 0:HF], Wl[l])
                load(wr_ext[0:F, l, 0:HF], Wr[l])
                load(wr_ext[F:F + 1, l, 0:HF], bl[l].rearrange("(a k) -> a k", a=1))
                load(att_row[:, l, :], att[l].rearrange("h f -> (h f)").partition_broadcast(P))
                flat = att[l].rearrange("h f -> (h f)")
                for q in range(3):
                    n = min(P, HF - q * P)
                    load(att_col[0:n, l, q:q + 1], flat[q * P:q * P + n].rearrange("(p a) -> p a", a=1))
                load(bl_cols[:, l, :], bl[l].rearrange("(h f) -> f h", f=F))
                load(bias_col[:, l:l + 1], gat_bias[l].rearrange("(p a) -> p a", a=1))
            load(wfc_ext[0:F, :], Wfc)
            load(wfc_ext[F:F + 1, :], bfc.rearrange("(a k) -> a k", a=1))
            load(ps_row[:, :], ps_w.rearrange("a f -> (a f)").partition_broadcast(P))
            load(cj[:, :], node_vec1.rearrange("(c p) a -> p (c a)", p=CN))
            load(ci[:, :], node_vec1_n2.rearrange("(w n) a -> n (w a)", n=WN))
            load(lin_tmp[F:F + 1, :], br[0].rearrange("(a k) -> a k", a=1))
            load(bias_tmp[F:F + 1, :], br[1].rearrange("(a k) -> a k", a=1))
            for l in range(2):
                sp.dma_start(dst_rows[l][W], zero_rows[:, :]).then_inc(zero_stored, 16)
            sp.wait_ge(zero_stored, 32)

            sp.wait_ge(counted, 2)
            R = n_rounds(sp)
            with sp.Fori(0, R) as r:
                hold(sp, tab_ready, r + 1)
                one = bass.ds(r, 1)
                sp.dma_start(src_tab[one].rearrange("a p i -> (a p) i"), src_o[:, :]).then_inc(tab_stored, 16)
                sp.dma_start(rel_tab[one].rearrange("a p i -> (a p) i"), rel_o[:, :]).then_inc(tab_stored, 16)
                sp.dma_start(win_tab[one], win_o[:, :]).then_inc(tab_stored, 16)
                sp.dma_start(first_tab[one], first_o[:, :]).then_inc(tab_stored, 16)
                sp.dma_start(relT_tab[one].rearrange("a (g p) e -> (a p) g e", p=IP),
                             relT_o[:, :, :]).then_inc(tab_stored, 16)
                hold(sp, tab_stored, (r + 1) * 80)
            barrier(sp, 1)

            def store_projections(l, c):
                ns = node_sem[l]
                hold(sp, ns["row_done"], c + 2)
                sp.dma_start(gat_rows[l][bass.ds(c * CN, CN), :], row_o[:, :]).then_inc(node_dma[l], 16)
                hold(sp, ns["parts_done"], c + 2)
                for v in range(5):
                    sp.dma_start(
                        dst_rows[l][bass.ds(c * 5 + v, 1)].rearrange("a (s n) z -> (a n) s z", n=WN),
                        parts[v * WN:(v + 1) * WN, :, :]).then_inc(node_dma[l], 16)
                hold(sp, node_dma[l], (c + 1) * 96)
                sp.sem_inc(ns["stored"], 1)

            def start_state(l):
                for h in range(H):
                    sp.dma_start(acc[h * WN:(h + 1) * WN, 0:W, :],
                                 gat_rows[l].rearrange("(w n) k -> n w k", n=WN)[:, :, ZC:ROW]
                                 ).then_inc(acc_init, 16)
                sp.wait_ge(acc_init, 16 * H * (l + 1))

            def load_table(g, r, bufs):
                one = bass.ds(r, 1)
                for buf, tab in bufs:
                    ap = tab[one]
                    sp.dma_start(buf[:, :], ap.rearrange("a p i -> (a p) i") if len(ap.shape) == 3 else ap
                                 ).then_inc(tab_loaded[g], 16)
                hold(sp, tab_loaded[g], (r + 1) * (16 * len(bufs)))

            def edges(l):
                def per_round(r, k):
                    hold(sp, es["acc_done3"], k)
                    load_table(l, r, ((src_s, src_tab), (win_s, win_tab)))
                    cur[0] = r

                def body(q, k, m, is_first, is_last):
                    for u in range(S):
                        col = q * ITER + u * U
                        wins = window_regs(sp, mybir.EngineType.SP, win_s, col, W)
                        hold(sp, es["oh_done"], k + (u - S + 1))
                        sp.dma_start(rel_b[:, u, :],
                                     relT_tab[bass.ds(cur[0], 1), bass.ds(col, U), :].rearrange(
                                         "a i e -> (a i e)").partition_broadcast(KO)
                                     ).then_inc(rel_loaded[u], 16)
                        hold(sp, es["z_done2"], k + (u - S + 1))
                        for j in range(U):
                            sp.dma_start(dst_w[0:KX, u, j, :],
                                         dst_rows[l][bass.ds(wins[j], 1)].rearrange("a k z -> (a k) z")
                                         ).then_inc(dst_loaded[u], 16)
                cur = [0]
                edge_rounds(sp, l, per_round, body)

            for l in range(2):
                with sp.Fori(0, NC) as c:
                    store_projections(l, c)
                barrier(sp, 2 + 3 * l)
                start_state(l)
                barrier(sp, 3 + 3 * l)
                edges(l)
                barrier(sp, 4 + 3 * l)
            sp.wait_ge(feat_done, 1)
            sp.dma_start(feat_rows.rearrange("(c p) f -> p c f", p=CN), xq[:, :, :]).then_inc(feat_stored, 16)
            sp.dma_start(resid_rows.rearrange("(c p) f -> p c f", p=CN), xs[:, :, :]).then_inc(feat_stored, 16)
            sp.wait_ge(feat_stored, 32)
            sp.dma_start(resid[:, :, :], resid_rows.rearrange("(w n) f -> n w f", n=WN)).then_inc(resid_loaded, 16)
            barrier(sp, 8)

            def per_round2(r, k):
                hold(sp, gs["acc2_done3"], k)
                load_table(2, r, ((src_s, src_tab), (rel_s, rel_tab), (win_s, win_tab), (first_s, first_tab)))

            def body2(q, k, m, is_first, is_last):
                for u in range(S):
                    col = q * ITER + u * U
                    firsts = window_regs(sp, mybir.EngineType.SP, first_s, col, LAST)
                    hold(sp, gs["pre_done"], k + (u - S + 1))
                    for j in range(U):
                        sp.dma_start(ea[:, u, j, :], edge_attr[bass.ds(firsts[j], P), :]
                                     ).then_inc(ea_loaded[u], 16)
            edge_rounds(sp, 0, per_round2, body2)
            sp.wait_ge(final_done, 1)
            sp.dma_start(out.rearrange("(w n) f -> n w f", n=WN), acc2[:, 0:W, :]).then_inc(out_stored, 16)
            sp.wait_ge(out_stored, 16)

        @block.gpsimd
        def _(pool):
            held[pool] = held_pool
            for s in list(es.values()) + list(gs.values()):
                pool.sem_inc(s, S)
            for ns in node_sem:
                for s in ns.values():
                    pool.sem_inc(s, 1)
            pool.wait_ge(counted, 2)
            barrier(pool, 1)

            def gathers(target, table, width, sems, done, used):
                def body(q, k, m, is_first, is_last):
                    for u in range(S):
                        pool.wait_ge(used, k + (u - S + 1))
                        hold(pool, done, k + (u + 1))
                        for j in range(U):
                            pool.indirect_dma_start(
                                out=target[:, u, j, :], out_offset=None, in_=table,
                                in_offset=bass.IndirectOffsetOnAxis(ap=idx[:, u, j:j + 1], axis=0)
                            ).then_inc(sems[u], 16)
                return body
            for l in range(2):
                barrier(pool, 2 + 3 * l)
                barrier(pool, 3 + 3 * l)
                edge_rounds(pool, l, lambda r, k: None,
                            gathers(rows, gat_rows[l][:, :], ROWP, gathered, es["idx_done"], es["sum_done"]))
                barrier(pool, 4 + 3 * l)
            barrier(pool, 8)
            edge_rounds(pool, 0, lambda r, k: None,
                        gathers(feat_g, feat_rows[:, :], F, gathered2, gs["idx2_done"], gs["sum2_done"]))

        @block.scalar
        def _(act):
            def root(n):
                act.wait_ge(var_done, n)
                act.activation(st[:, 2, :], st[:, 1, :], ACT.Sqrt).then_inc(sd_done, 1)

            act.wait_ge(counted, 2)
            barrier(act, 1)
            root(1)

            def project(l, c):
                ns = node_sem[l]
                act.wait_ge(ns["proj_done"], c + 2)
                act.wait_ge(ns["stored"], c + 1)
                act.wait_ge(ns["loop_done"], c + 1)
                act.activation(row_o[:, 0:ROW], ps[0:CN, 0, 0:ROW], ACT.Copy).then_inc(ns["row_done"], 1)

            def turn_mean(ns, c):
                act.wait_ge(ns["mean_turned"], c + 2)
                act.wait_ge(ns["mixed"], c + 1)
                act.activation(mean_T[:, 0:4, :].rearrange("p v k -> p (v k)"), ps[0:F, 4, 0:4 * HW], ACT.Copy)
                act.activation(mean_T[:, 4, :], ps[0:F, 5, 0:HW], ACT.Copy).then_inc(ns["mean_T_done"], 1)

            def mix(ns, l, c, used):
                act.wait_ge(ns["mixed"], c + 2)
                act.wait_ge(used, c + 1)
                act.activation(h_T[0:F, :], ps[0:F, 6, 0:CN], ACT.Relu, bias=out_bias[:, l:l + 1],
                               scale=1.0 / H).then_inc(ns["h_T_done"], 1)

            def edges(l):
                def make_idx(k, u, table_col):
                    act.wait_ge(es["sum_done"], k + (u - S + 1))
                    act.copy(idx[:, u % S, :], src_s[:, bass.ds(table_col, U)]).then_inc(es["idx_done"], 1)

                def per_round(r, k):
                    act.wait_ge(tab_loaded[l], (r + 1) * 32)
                    for u in range(AHEAD):
                        make_idx(k, u, u * U)

                def exps(k, u, hh):
                    b = u % 2
                    act.wait_ge(es[f"nm_done{hh}"], k + (u + 1))
                    act.wait_ge(es["p_turned"], k + (u - 1))
                    for j in (2 * hh, 2 * hh + 1):
                        i = act.activation(p_T[:, b, j, :], ps[0:HW, logit_bank(u, hh), (j % 2) * P:(j % 2 + 1) * P], ACT.Exp,
                                           bias=nm[:, b, j:j + 1])
                    if hh == 0:
                        i.then_inc(es["p_half_done"], 1)
                    else:
                        i.then_inc(es["p_done"], 1)
                        act.wait_ge(es["acc_done3"], k + (u - 1))
                        act.activation(scale[:, b, :], dm[:, b, :], ACT.Exp).then_inc(es["scale_done"], 1)

                def copy_p(k, u):
                    act.wait_ge(es["p_turned"], k + (u + 1))
                    act.wait_ge(es["sum_done"], k + u)
                    act.copy(p_e[:, :, :].rearrange("p j k -> p (j k)"), ps[:, 5, 0:U * HW]
                             ).then_inc(es["p_e_done"], 1)

                def body(q, k, m, is_first, is_last):
                    for u in range(S + 2 if is_last else S):
                        b = u % 2
                        if u < S:
                            act.wait_ge(es["logit_done1"], k + (u - 1))
                            for z in range(2):
                                act.wait_ge(es[f"z_done{z}"], k + (u + 1))
                                act.activation(relu[:, b, z, :], ps[:, z, :], ACT.Relu
                                               ).then_inc(es[f"relu_done{z}"], 1)
                        if not (is_first and u < 2):
                            exps(k, u - 2, 1)
                            copy_p(k, u - 2)
                        if not (is_first and u < 1) and u <= S:
                            exps(k, u - 1, 0)
                        if not (is_last and u + AHEAD >= S):
                            make_idx(k, u + AHEAD, q * ITER + (u + AHEAD) * U)
                edge_rounds(act, l, per_round, body)

            ns = node_sem[0]
            with act.Fori(0, NC) as c:
                act.wait_ge(ns["h_turned"], c + 2)
                act.wait_ge(ns["proj_done"], c + 1)
                act.activation(h_T[0:F, :], ps[0:F, 2, 0:CN], ACT.Copy).then_inc(ns["h_T_done"], 1)
                project(0, c)
            barrier(act, 2)
            barrier(act, 3)
            edges(0)
            barrier(act, 4)
            ns = node_sem[1]
            with act.Fori(0, NC) as c:
                turn_mean(ns, c)
                mix(ns, 0, c, ns["proj_done"])
                project(1, c)
            barrier(act, 5)
            barrier(act, 6)
            edges(1)
            barrier(act, 7)
            ns = node_sem[2]
            with act.Fori(0, NC) as c:
                turn_mean(ns, c)
                mix(ns, 1, c, ns["fc_done"])
            root(2)
            barrier(act, 8)

            def make_idx2(k, u, table_col):
                act.wait_ge(gs["sum2_done"], k + (u - S + 1))
                act.copy(idx[:, u % S, :], src_s[:, bass.ds(table_col, U)]).then_inc(gs["idx2_done"], 1)

            def per_round2(r, k):
                act.wait_ge(tab_loaded[2], (r + 1) * 64)
                for u in range(AHEAD):
                    make_idx2(k, u, u * U)

            def body2(q, k, m, is_first, is_last):
                for u in range(S):
                    act.wait_ge(gs["pre_done"], k + (u + 1))
                    act.wait_ge(gs["gate_done"], k + (u - 1))
                    act.activation(pa[:, u % 2, :], pre[:, u % 2, :], ACT.Sigmoid).then_inc(gs["pa_done"], 1)
                    if not (is_last and u + AHEAD >= S):
                        make_idx2(k, u + AHEAD, q * ITER + (u + AHEAD) * U)
            edge_rounds(act, 0, per_round2, body2)

        @block.tensor
        def _(pe):
            held[pe] = held_pe
            mm = pe.matmul
            ident = const("ident")

            def turn(o, i, rows_, start=True, stop=True):
                return mm(o, i, cst[0:rows_, at["ident"][0]:at["ident"][0] + rows_], start=start, stop=stop,
                          is_transpose=True)

            pe.wait_ge(counted, 1)
            mm(ps[:, 0, 0:TC], const("before"), cnt[:, :], start=True, stop=False)
            mm(ps[:, 0, 0:TC], const("ones"), fl_f[:, 0:TC], start=False, stop=True)
            mm(ps[:, 1, 0:1], const("ones"), cum[:, TC - 1:TC], start=True, stop=True).then_inc(prefix_done, 1)
            pe.wait_ge(counted, 2)
            R = n_rounds(pe)
            with pe.Fori(0, R) as r:
                for t in range(TC):
                    pe.wait_ge(picked, r * TC + (t + 1))
                    for a, lhs in enumerate((src_f[:, t, :], dst_f[:, t, 0:P], win_base[:, t, :],
                                             cst[:, at["tile_col"][0] + t:at["tile_col"][0] + t + 1])):
                        for hh in range(2):
                            m = mm(ps[0:P if a < 3 else 1, 2 * a + hh, 0:HALF], lhs,
                                   pick[:, t, hh * HALF:(hh + 1) * HALF], start=(t == 0), stop=(t == TC - 1))
                m.then_inc(expanded, 1)
                pe.wait_ge(moved, r + 1)
                for g in range(IG):
                    for t in range(TC):
                        m = mm(ps[0:IP, g // 3, (g % 3) * (P + 1):(g % 3 + 1) * (P + 1)],
                               pick[:, t, g * IP:(g + 1) * IP], dst_f[:, t, :], start=(t == 0), stop=(t == TC - 1))
                m.then_inc(expandedT, 1)
            barrier(pe, 1)

            def project(l, c):
                ns = node_sem[l]
                pe.wait_ge(ns["h_T_done"], c + 2)
                pe.wait_ge(ns["row_done"], c + 1)
                pe.wait_ge(ns["loop_spread"], c + 1)
                mm(ps[0:CN, 0, 0:ROW], h_T[:, :], wl_ext[:, l, :], start=True, stop=True)
                mm(ps[0:CN, 1, 0:ZC], h_T[:, :], wr_ext[:, l, :], start=True, stop=True
                   ).then_inc(ns["proj_done"], 1)

            def spread_loops(l, c):
                ns = node_sem[l]
                pe.wait_ge(ns["loop_spread"], c + 2)
                pe.wait_ge(ns["loop_done"], c + 1)
                mm(ps[0:HW, 3, 0:5], d_loop[:, :, :].rearrange("p h n -> p (h n)"), const("winsel", CN),
                   start=True, stop=True).then_inc(ns["loop_turned"], 1)

            def turn_mean(ns, c):
                pe.wait_ge(ns["mean_done"], c + 2)
                hold(pe, ns["mean_T_done"], c + 1)
                for v in range(5):
                    m = turn(ps[0:F, 4 + v // 4, (v % 4) * HW:(v % 4 + 1) * HW], mean_x[:, v, :], HW)
                m.then_inc(ns["mean_turned"], 1)

            def mix(ns, l, c):
                pe.wait_ge(ns["mean_T_done"], c + 2)
                hold(pe, ns["h_T_done"], c + 1)
                for h in range(H):
                    m = mm(ps[0:F, 6, 0:CN], wl_ext[0:F, l, h * F:(h + 1) * F],
                           mean_T[:, :, h * WN:(h + 1) * WN], start=(h == 0), stop=(h == H - 1))
                m.then_inc(ns["mixed"], 1)

            def edges(l):
                def z_step(k, m_, u):
                    pe.wait_ge(gathered[u], m_ * (16 * U))
                    pe.wait_ge(dst_loaded[u], m_ * (16 * U))
                    pe.wait_ge(es["oh_done"], k + (u + 1))
                    for z in range(3):
                        n = ZQ[z]
                        pe.wait_ge(es[f"relu_done{z}"], k + u)
                        for j in range(U):
                            o = ps[0:n, z, j * P:(j + 1) * P]
                            turn(o, rows[:, u, j, z * P:z * P + n], P, stop=False)
                            m = mm(o, dst_w[:, u, j, z * P:z * P + n], oh[:, u % 3, j * P:(j + 1) * P],
                                   start=False, stop=True)
                        m.then_inc(es[f"z_done{z}"], 1)

                def logits(k, u, hh):
                    b = u % 2
                    if hh == 0:
                        for z in range(3):
                            pe.wait_ge(es[f"relu_done{z}"], k + (u + 1))
                        pe.wait_ge(es["p_done"], k + (u - 1))
                    else:
                        pe.wait_ge(es["p_half_done"], k + u)
                    cols = slice(hh * 2 * P, (hh + 1) * 2 * P)
                    o = ps[0:HW, logit_bank(u, hh), 0:2 * P]
                    mm(o, outside[0:KO, :], oh[:, u % 3, cols], start=True, stop=False)
                    for z in range(3):
                        n = ZQ[z]
                        m = mm(o, att_mat[0:n, l, z, :], relu[0:n, b, z, cols], start=False, stop=(z == 2))
                    m.then_inc(es[f"logit_done{hh}"], 1)

                def turn_p(k, u):
                    pe.wait_ge(es["p_done"], k + (u + 1))
                    pe.wait_ge(es["p_e_done"], k + u)
                    for j in range(U):
                        m = turn(ps[:, 5, j * HW:(j + 1) * HW], p_T[:, u % 2, j, :], HW)
                    m.then_inc(es["p_turned"], 1)

                def sums(k, u):
                    pe.wait_ge(es["p_e_done"], k + (u + 1))
                    pe.wait_ge(es["acc_done3"], k + u)
                    for j in range(U):
                        m = mm(ps[0:HW, 6, j * (F + 1):(j + 1) * (F + 1)], p_e[:, j, :],
                               rows[:, u % S, j, ZC:ROW], start=True, stop=True)
                    m.then_inc(es["sum_done"], 1)

                def body(q, k, m, is_first, is_last):
                    for u in range(S + 2 if is_last else S):
                        lag1 = not (is_first and u < 1) and u <= S
                        lag2 = not (is_first and u < 2)
                        if u < S:
                            z_step(k, m, u)
                        if lag1:
                            logits(k, u - 1, 0)
                        if lag2:
                            turn_p(k, u - 2)
                        if lag1:
                            logits(k, u - 1, 1)
                        if lag2:
                            sums(k, u - 2)
                edge_rounds(pe, l, lambda r, k: None, body)

            ns = node_sem[0]
            with pe.Fori(0, NC) as c:
                pe.wait_ge(ns["h_node_done"], c + 2)
                hold(pe, ns["h_T_done"], c + 1)
                turn(ps[0:F, 2, 0:CN], h_node[:, :], CN).then_inc(ns["h_turned"], 1)
                project(0, c)
                spread_loops(0, c)
            barrier(pe, 2)
            barrier(pe, 3)
            edges(0)
            barrier(pe, 4)
            ns = node_sem[1]
            with pe.Fori(0, NC) as c:
                turn_mean(ns, c)
                mix(ns, 0, c)
                project(1, c)
                spread_loops(1, c)
            barrier(pe, 5)
            barrier(pe, 6)
            edges(1)
            barrier(pe, 7)
            ns = node_sem[2]
            with pe.Fori(0, NC) as c:
                turn_mean(ns, c)
                mix(ns, 1, c)
                pe.wait_ge(ns["h_T_done"], c + 2)
                pe.wait_ge(ns["resid_done"], c + 1)
                mm(ps[0:CN, 7, 0:F], h_T[:, :], wfc_ext[:, :], start=True, stop=True).then_inc(ns["fc_done"], 1)
            barrier(pe, 8)

            def body2(q, k, m, is_first, is_last):
                for u in range(S):
                    b = u % 2
                    pe.wait_ge(gathered2[u], m * (16 * U))
                    pe.wait_ge(gs["gate_done"], k + (u + 1))
                    pe.wait_ge(gs["acc2_done3"], k + (u - 1))
                    for j in range(U):
                        i = mm(ps[0:WN, b, j * F:(j + 1) * F], gate[:, b, j, :], feat_g[:, u, j, :],
                               start=True, stop=True)
                    i.then_inc(gs["sum2_done"], 1)
            edge_rounds(pe, 0, lambda r, k: None, body2)

        @block.vector
        def _(dve):
            TT, TS, STT, CP = dve.tensor_tensor, dve.tensor_scalar, dve.scalar_tensor_tensor, dve.tensor_copy

            def settle():
                dve.drain()

            dve.memset(src_i[:, TC - 1, :], 0)
            dve.memset(dst_i[:, TC - 1, :], -1)
            dve.memset(zero_rows[:, :], 0.0)
            dve.memset(wl_ext[:, :, :], 0.0)
            dve.memset(att_col[:, :, :], 0.0)
            dve.memset(h_T[:, :], 1.0)
            dve.memset(row_o[:, :], 0.0)
            dve.memset(neg_max[:, :], 0.0)
            settle()
            dve.memset(cum[:, :], 1.0).then_inc(zeroed, 1)
            dve.wait_ge(loaded, n_loads[0])

            CP(dst_f[:, :, 0:P], dst_i[:, :, :])
            CP(src_f[:, :, :], src_i[:, :, :])
            settle()
            TS(dst_y[:, :, :], dst_f[:, :, 0:P], 0.0, 1.0e6, ALU.is_lt, ALU.mult)
            dve.tensor_reduce(ext[:, 1, :], dst_f[:, :, 0:P], AX.X, ALU.max)
            settle()
            TT(dst_y[:, :, :], dst_y[:, :, :], dst_f[:, :, 0:P], ALU.add)
            settle()
            dve.tensor_reduce(ext[:, 0, :], dst_y[:, :, :], AX.X, ALU.min)
            settle()

            def floor_div(o, a, d, n):
                TS(fl_i[:, 0:n], a, 1.0 / d, None, ALU.mult)
                settle()
                CP(fl_f[:, 0:n], fl_i[:, 0:n])
                settle()
                STT(fl_r[:, 0:n], fl_f[:, 0:n], -float(d), a, ALU.mult, ALU.add)
                settle()
                TS(fl_a[:, 0:n], fl_r[:, 0:n], float(d), None, ALU.is_ge)
                TS(fl_r[:, 0:n], fl_r[:, 0:n], 0.0, None, ALU.is_lt)
                settle()
                TT(fl_a[:, 0:n], fl_a[:, 0:n], fl_r[:, 0:n], ALU.subtract)
                settle()
                TT(o, fl_a[:, 0:n], fl_f[:, 0:n], ALU.add)
                settle()

            floor_div(extw[:, :, :].rearrange("p a c -> p (a c)"), ext[:, :, :].rearrange("p a c -> p (a c)"),
                      WN, 2 * TC)
            TT(cnt[:, :], extw[:, 1, :], extw[:, 0, :], ALU.subtract)
            settle()
            TS(cnt[:, :], cnt[:, :], 1.0, 0.0, ALU.add, ALU.max)
            settle()
            dve.tensor_tensor_scan(cum[:, :], cst[:, at["ones"][0]:at["ones"][0] + TC], cnt[:, :], 0.0,
                                   ALU.mult, ALU.add)
            settle()
            TT(fl_f[:, 0:TC], cum[:, :], cnt[:, :], ALU.subtract)
            settle()
            dve.memset(fl_r[:, :], 0.0).then_inc(counted, 1)
            dve.wait_ge(prefix_done, 1)
            CP(first[:, :], ps[:, 0, 0:TC])
            TS(rounds_f[:, :], ps[:, 1, 0:1], float(ITEMS - 1), None, ALU.add)
            settle()
            TT(end[:, :], first[:, :], cnt[:, :], ALU.add)
            TT(dst_f[:, :, P], extw[:, 0, :], first[:, :], ALU.subtract)
            floor_div(rounds_w[:, :], rounds_f[:, :], ITEMS, 1)
            CP(rounds_i[:, :], rounds_w[:, :])
            settle()
            dve.memset(fl_r[:, :], 0.0).then_inc(counted, 1)

            R = n_rounds(dve)
            with dve.Fori(0, R) as r:
                CP(win_base[:, :, :], dst_f[:, :, P:P + 1].to_broadcast([P, TC, P]))
                settle()
                for t in range(TC):
                    TS(ge[:, :], const("item_row"), first[:, t:t + 1], None, ALU.is_ge)
                    settle()
                    STT(pick[:, t, :], const("item_row"), end[:, t:t + 1], ge[:, :], ALU.is_lt, ALU.mult
                        ).then_inc(picked, 1)
                    settle()
                dve.wait_ge(expanded, r + 1)

                def halves(a, n=P):
                    return ps[0:n, 2 * a:2 * a + 2, 0:HALF]

                def two(ap):
                    return ap.rearrange("p (a b) -> p a b", a=2)
                CP(two(src_o[:, :]), halves(0))
                TT(two(win_f[:, :]), halves(2), two(const("item_row")), ALU.add)
                TS(two(first_f[:, :]), halves(3, 1), float(P), float(LAST), ALU.mult, ALU.min)
                settle()
                TS(win_f[:, :], win_f[:, :], float(W), None, ALU.min)
                settle()
                STT(two(rel_o[:, :]), two(win_f[:, :]), -float(WN), halves(1), ALU.mult, ALU.add)
                CP(win_o[:, :], win_f[0:1, :])
                CP(first_o[:, :], first_f[:, :])
                settle()
                dve.memset(fl_r[:, :], 0.0).then_inc(moved, 1)
                dve.wait_ge(expandedT, r + 1)
                for g in range(IG):
                    o = ps[0:IP, g // 3, (g % 3) * (P + 1):(g % 3 + 1) * (P + 1)]
                    TT(win_c[:, g:g + 1], o[:, P:P + 1], const("item_col", IP)[:, g:g + 1], ALU.add)
                settle()
                TS(win_c[:, :], win_c[:, :], float(W), -float(WN), ALU.min, ALU.mult)
                settle()
                for g in range(IG):
                    o = ps[0:IP, g // 3, (g % 3) * (P + 1):(g % 3 + 1) * (P + 1)]
                    TS(relT_f[:, g, :], o[:, 0:P], win_c[:, g:g + 1], None, ALU.add)
                settle()
                TS(relT_m[:, :, :], relT_f[:, :, :], 0.0, None, ALU.is_ge)
                settle()
                STT(relT_m[:, :, :], relT_f[:, :, :], float(WN - 1), relT_m[:, :, :], ALU.is_le, ALU.mult)
                settle()
                STT(relT_f[:, :, :], relT_f[:, :, :], float(WN), relT_m[:, :, :], ALU.subtract, ALU.mult)
                settle()
                TS(relT_o[:, :, :], relT_f[:, :, :], float(WN), None, ALU.add)
                TS(first[:, :], first[:, :], -float(ITEMS), None, ALU.add)
                TS(end[:, :], end[:, :], -float(ITEMS), None, ALU.add)
                TS(dst_f[:, :, P], dst_f[:, :, P], float(ITEMS), None, ALU.add)
                settle()
                dve.memset(fl_r[:, :], 0.0).then_inc(tab_ready, 1)
                dve.wait_ge(tab_stored, (r + 1) * 80)

            CP(outside[:, :], const("outside"))
            TT(wr_ext[F:F + 1, 0, 0:HF], wr_ext[F:F + 1, 0, 0:HF], lin_tmp[F:F + 1, :], ALU.add)
            TT(wr_ext[F:F + 1, 1, 0:HF], wr_ext[F:F + 1, 1, 0:HF], bias_tmp[F:F + 1, :], ALU.add)
            for l in range(2):
                CP(wl_ext[:, l, ZC:ROW], cst[0:F + 1, at["ident"][0]:at["ident"][0] + F + 1])
                dve.tensor_reduce(out_bias[:, l:l + 1], bl_cols[:, l, :], AX.X, ALU.add)
                for z in range(3):
                    TS(att_mat[:, l, z, :], cst[:, at["headmask"][0] + z * HW:at["headmask"][0] + (z + 1) * HW],
                       att_col[:, l, z:z + 1], 0.8, ALU.mult, ALU.mult)
            settle()
            for l in range(2):
                TT(att_mat[:, l, 2, :], att_mat[:, l, 2, :], const("linsel"), ALU.add)
                STT(out_bias[:, l:l + 1], out_bias[:, l:l + 1], 1.0 / H, bias_col[:, l:l + 1], ALU.mult, ALU.add)
                for w_ext in (wl_ext, wr_ext):
                    TT(lin_tmp[:, :], w_ext[:, l, 0:HF], att_row[0:F + 1, l, :], ALU.mult)
                    settle()
                    dve.tensor_reduce(lin_sum[:, :], lin_tmp[:, :].rearrange("p (h f) -> p h f", h=H), AX.X, ALU.add)
                    settle()
                    TS(w_ext[:, l, HF:HF + H], lin_sum[:, :], 0.2, None, ALU.mult)
                    TS(w_ext[:, l, HF + H:ZC], lin_sum[:, :], -0.2, None, ALU.mult)
                    settle()
            barrier(dve, 1)
            dve.memset(dst_w[:, :, :, :], 0.0)
            dve.memset(acc[:, :, :], 1.0)

            def center(n):
                dve.tensor_reduce(st[:, 0, :], xs[:, :, :], AX.X, ALU.add)
                settle()
                TS(st[:, 0, :], st[:, 0, :], 1.0 / F, None, ALU.mult)
                settle()
                TT(xc[:, :, :], xs[:, :, :], st[:, 0, :].unsqueeze(2).to_broadcast([CN, NC, F]), ALU.subtract)
                settle()
                TT(xq[:, :, :], xc[:, :, :], xc[:, :, :], ALU.mult)
                settle()
                dve.tensor_reduce(st[:, 0, :], xq[:, :, :], AX.X, ALU.add)
                settle()
                TS(st[:, 1, :], st[:, 0, :], 1.0 / F, EPS, ALU.mult, ALU.add).then_inc(var_done, 1)
                dve.wait_ge(sd_done, n)
                dve.reciprocal(st[:, 3, :], st[:, 2, :])
                settle()

            def project(l, c):
                ns = node_sem[l]
                r_ps = ps[0:CN, 1, :]
                dve.wait_ge(ns["proj_done"], c + 2)
                dve.wait_ge(ns["stored"], c + 1)
                CP(parts[:, 0, :], r_ps[:, 0:ZC])
                settle()
                TT(rest[:, :], r_ps[:, 0:ZC], parts[:, 0, :], ALU.subtract)
                settle()
                CP(parts[:, 1, :], rest[:, :])
                settle()
                TT(parts[:, 2, :], rest[:, :], parts[:, 1, :], ALU.subtract).then_inc(ns["parts_done"], 1)
                dve.wait_ge(ns["row_done"], c + 2)
                TT(z_loop[:, :], row_o[:, 0:HF], r_ps[:, 0:HF], ALU.add)
                TT(s_loop[:, 0, :], row_o[:, HF:HF + H], r_ps[:, HF:HF + H], ALU.add)
                settle()
                STT(z_loop[:, :], z_loop[:, :], 0.0, att_row[0:CN, l, :], ALU.max, ALU.mult)
                settle()
                dve.tensor_reduce(s_loop[:, 1, :], z_loop[:, :].rearrange("p (h f) -> p h f", h=H), AX.X, ALU.add)
                settle()
                STT(s_loop[:, 2, :], s_loop[:, 1, :], 0.8, s_loop[:, 0, :], ALU.mult, ALU.add)
                settle()
                dve.wait_ge(ns["loop_turned"], c + 1)
                TT(d_loop[:, :, :], s_loop[:, 2, :].unsqueeze(2).to_broadcast([CN, H, WN]),
                   const("nodesel", CN).unsqueeze(1).to_broadcast([CN, H, WN]), ALU.mult
                   ).then_inc(ns["loop_spread"], 1)
                dve.wait_ge(ns["loop_turned"], c + 2)
                TS(neg_max[:, bass.ds(c * 5, 5)], ps[0:HW, 3, 0:5], -1.0, None, ALU.mult
                   ).then_inc(ns["loop_done"], 1)

            def mean(ns, c):
                dve.reciprocal(inv_l[:, :], acc[:, bass.ds(c * 5, 5), F])
                settle()
                dve.wait_ge(ns["mean_turned"], c + 1)
                TT(mean_x[:, :, :], acc[:, bass.ds(c * 5, 5), 0:F],
                   inv_l[:, :].unsqueeze(2).to_broadcast([HW, 5, F]), ALU.mult).then_inc(ns["mean_done"], 1)

            def edges(l):
                def one_hot(k, m, u):
                    dve.wait_ge(rel_loaded[u % S], (m + u // S) * 16)
                    dve.wait_ge(es["logit_done1"], k + (u - 2))
                    TS(oh[:, u % 3, :], rel_b[:, u % S, :], const("slot", KO), None, ALU.is_equal
                       ).then_inc(es["oh_done"], 1)

                def relu_last(k, u):
                    n = ZQ[2]
                    dve.wait_ge(es["logit_done1"], k + (u - 1))
                    dve.wait_ge(es["z_done2"], k + (u + 1))
                    TS(relu[0:n, u % 2, 2, :], ps[0:n, 2, :], 0.0, None, ALU.max).then_inc(es["relu_done2"], 1)

                def maxima(k, u, hh, wins):
                    b = u % 2
                    dve.wait_ge(es["scale_done"], k + (u - 1))
                    dve.wait_ge(es[f"logit_done{hh}"], k + (u + 1))
                    dve.tensor_reduce(neg_item[:, b, 2 * hh:2 * hh + 2],
                                      ps[0:HW, logit_bank(u, hh), 0:2 * P].rearrange(
                                          "p (j e) -> p j e", j=2), AX.X, ALU.max, negate=True
                                      ).then_inc(es[f"max_done{hh}"], 1)
                    dve.wait_ge(es[f"max_done{hh}"], k + (u + 1))
                    for j in (2 * hh, 2 * hh + 1):
                        m = neg_item[:, b, j:j + 1]
                        state = neg_max[:, bass.ds(wins[j], 1)]
                        dve.wait_ge(es[f"state_done{(j - 1) % U}"], k + (u if j == 0 else u + 1))
                        TT(nm[:, b, j:j + 1], m, state, ALU.min)
                        i = TS(dm[:, b, j:j + 1], m, state, 0.0, ALU.subtract, ALU.min)
                        if j % 2:
                            i.then_inc(es[f"nm_done{hh}"], 1)
                        TT(state, m, state, ALU.min).then_inc(es[f"state_done{j}"], 1)

                def take_sums(k, u, wins):
                    dve.wait_ge(es["sum_done"], k + (u + 1))
                    dve.wait_ge(es["scale_done"], k + (u + 1))
                    for j in range(U):
                        a = acc[:, bass.ds(wins[j], 1), :].rearrange("p a f -> p (a f)")
                        dve.wait_ge(es[f"acc_done{(j - 1) % U}"], k + (u if j == 0 else u + 1))
                        STT(a, a, scale[:, u % 2, j:j + 1], ps[0:HW, 6, j * (F + 1):(j + 1) * (F + 1)],
                            ALU.mult, ALU.add).then_inc(es[f"acc_done{j}"], 1)

                def per_round(r, k):
                    dve.wait_ge(tab_loaded[l], (r + 1) * 32)

                def body(q, k, m, is_first, is_last):
                    col = q * ITER
                    if is_first:
                        one_hot(k, m, 0)
                        one_hot(k, m, 1)
                    wins = {}
                    for u in range(S + 2 if is_last else S):
                        lag1 = not (is_first and u < 1) and u <= S
                        lag2 = not (is_first and u < 2)
                        for v in (u - 2, u - 1):
                            if v not in wins and (not is_first or v >= 0) and v < S:
                                wins[v] = window_regs(dve, mybir.EngineType.DVE, win_s, col + v * U, W)
                        if u < S:
                            relu_last(k, u)
                        if lag1:
                            maxima(k, u - 1, 0, wins[u - 1])
                            maxima(k, u - 1, 1, wins[u - 1])
                        if lag2:
                            take_sums(k, u - 2, wins[u - 2])
                        if not (is_last and u + 2 >= S):
                            one_hot(k, m, u + 2)
                edge_rounds(dve, l, per_round, body)

            center(1)
            ns = node_sem[0]
            with dve.Fori(0, NC) as c:
                dve.wait_ge(ns["h_turned"], c + 1)
                TS(h_node[:, :], xc[:, bass.ds(c, 1), :].rearrange("p a f -> p (a f)"),
                   st[:, 3, bass.ds(c, 1)], 0.0, ALU.mult, ALU.max).then_inc(ns["h_node_done"], 1)
                project(0, c)
            barrier(dve, 2)
            barrier(dve, 3)
            edges(0)
            barrier(dve, 4)
            ns = node_sem[1]
            with dve.Fori(0, NC) as c:
                mean(ns, c)
                project(1, c)
            barrier(dve, 5)
            barrier(dve, 6)
            edges(1)
            barrier(dve, 7)
            ns = node_sem[2]
            with dve.Fori(0, NC) as c:
                mean(ns, c)
                dve.wait_ge(ns["fc_done"], c + 2)
                xr = xs[:, bass.ds(c, 1), :].rearrange("p a f -> p (a f)")
                TT(xr, xr, ps[0:CN, 7, 0:F], ALU.add).then_inc(ns["resid_done"], 1)
            dve.memset(acc2[:, :, :], 0.0)
            settle()
            center(2)
            TT(xq[:, :, :], xc[:, :, :], st[:, 3, :].unsqueeze(2).to_broadcast([CN, NC, F]), ALU.mult)
            settle()
            TS(xq[:, :, :], xq[:, :, :], 0.0, None, ALU.max)
            settle()
            TT(xq[:, :, :], xq[:, :, :], cj[:, :].unsqueeze(2).to_broadcast([CN, NC, F]), ALU.mult
               ).then_inc(feat_done, 1)
            barrier(dve, 8)

            def product(k, m, u):
                dve.wait_ge(ea_loaded[u % S], (m + u // S) * (16 * U))
                dve.wait_ge(gs["pa_done"], k + (u - 1))
                e = ea[:, u % S, :, :]
                TT(e, e, ps_row[:, :].unsqueeze(1).to_broadcast([P, U, F]), ALU.mult).then_inc(gs["prod_done"], 1)
                dve.wait_ge(gs["prod_done"], k + (u + 1))
                dve.tensor_reduce(pre[:, u % 2, :], e, AX.X, ALU.add).then_inc(gs["pre_done"], 1)

            def gates(k, u, col):
                TT(oh2[:, :, :], rel_s[:, bass.ds(col, U)].unsqueeze(2).to_broadcast([P, U, WN]),
                   cst[:, at["item_row"][0]:at["item_row"][0] + WN].unsqueeze(1).to_broadcast([P, U, WN]),
                   ALU.is_equal).then_inc(gs["oh2_done"], 1)
                dve.wait_ge(gs["oh2_done"], k + (u + 1))
                dve.wait_ge(gs["pa_done"], k + (u + 1))
                dve.wait_ge(gs["sum2_done"], k + (u - 1))
                TT(gate[:, u % 2, :, :], oh2[:, :, :], pa[:, u % 2, :].unsqueeze(2).to_broadcast([P, U, WN]),
                   ALU.mult).then_inc(gs["gate_done"], 1)

            def take_sums2(k, u, col):
                wins = window_regs(dve, mybir.EngineType.DVE, win_s, col, W)
                dve.wait_ge(gs["sum2_done"], k + (u + 1))
                for j in range(U):
                    a = acc2[:, bass.ds(wins[j], 1), :].rearrange("p a f -> p (a f)")
                    dve.wait_ge(gs[f"acc2_done{(j - 1) % U}"], k + (u if j == 0 else u + 1))
                    TT(a, a, ps[0:WN, u % 2, j * F:(j + 1) * F], ALU.add).then_inc(gs[f"acc2_done{j}"], 1)

            def per_round2(r, k):
                dve.wait_ge(tab_loaded[2], (r + 1) * 64)

            def body2(q, k, m, is_first, is_last):
                if is_first:
                    product(k, m, 0)
                for u in range(S):
                    if not (is_last and u == S - 1):
                        product(k, m, u + 1)
                    gates(k, u, q * ITER + u * U)
                    if not (is_first and u == 0):
                        take_sums2(k, u - 1, q * ITER + (u - 1) * U)
                if is_last:
                    take_sums2(k, S - 1, q * ITER + (S - 1) * U)
            edge_rounds(dve, 0, per_round2, body2)
            settle()
            dve.wait_ge(resid_loaded, 16)
            TT(acc2[:, 0:W, :], acc2[:, 0:W, :], ci[:, :].unsqueeze(2).to_broadcast([WN, W, F]), ALU.mult)
            settle()
            TT(acc2[:, 0:W, :], acc2[:, 0:W, :], resid[:, :, :], ALU.add).then_inc(final_done, 1)


INPUTS = ["x", "src", "dst", "edge_attr_64", "node_vec1", "node_vec1_n2",
          "L0_gnn_W1l", "L0_gnn_b1l", "L0_gnn_W1r", "L0_gnn_b1r", "L0_gnn_att1", "L0_gnn_bias1",
          "L0_gnn_W2l", "L0_gnn_b2l", "L0_gnn_W2r", "L0_gnn_b2r", "L0_gnn_att2", "L0_gnn_bias2",
          "L0_gnn_Wfc", "L0_gnn_bfc", "L1_gnn_ps_w"]


def kernel(**inputs):
    import concourse.bacc as bacc
    from concourse.bass_utils import run_bass_kernel_spmd

    nc = bacc.Bacc("TRN2", target_bir_lowering=False, num_devices=1)
    arrays, args = {}, []
    for name in INPUTS + ["constants"]:
        a = shape_constants() if name == "constants" else np.ascontiguousarray(inputs[name])
        arrays[f"in_{name}"] = a
        args.append(nc.dram_tensor(f"in_{name}", a.shape, mybir.dt.from_np(a.dtype), kind="ExternalInput").ap())
    out = nc.dram_tensor("out_0", (N, F), F32, kind="ExternalOutput").ap()
    build_program(nc, *args, out)
    result = run_bass_kernel_spmd(nc, [arrays], core_ids=[0])
    return result.results[0]["out_0"]
```

```python
from contextlib import ExitStack

import numpy as np

import concourse.bass as bass
from concourse import mybir

P = 128
N = 3125
E = 103125
F = 64
H = 5
HF = H * F
WN = 25
W = N // WN
HW = H * WN
CN = 5 * WN
NC = N // CN
UC = 5
LIN = 2 * H
ZC = HF + LIN
NH = WN + 1
ZE = ZC + NH
ROW = ZE + F + 1
ROWP = ROW + 1
ZQ = [P, P, ZE - 2 * P]
T = -(-E // P)
TC = -(-T // P)
LAST = E - P
U = 4
S = 6
AHEAD = 4
ITER = U * S
NIT = -(-(T + W - 1) // ITER)
ITEMS = NIT * ITER
HALF = ITEMS // 2
SPAN = 32
TROWS = TC * P
TNIT = -(-T // ITER)
IG = 8
IP = ITEMS // IG
RMAX = -(-(T * W) // ITEMS)
KX = 3 * WN
KO = KX + 1
BIG = float(2 ** 60)
EPS = 1e-5

F32 = mybir.dt.float32
BF16 = mybir.dt.bfloat16
I32 = mybir.dt.int32
ALU = mybir.AluOpType
ACT = mybir.ActivationFunctionType
AX = mybir.AxisListType


def constant_columns():
    widths = [("ident", P), ("before", P), ("ones", P), ("headmask", 3 * HW), ("linsel", HW),
              ("hotcols", NH), ("nodesel", WN), ("winsel", 5), ("slot", 1), ("item_col", IG),
              ("item_row", ITEMS)]
    at, c = {}, 0
    for name, w in widths:
        at[name] = (c, w)
        c += w
    return at, c


def shape_constants():
    at, total = constant_columns()
    a = np.zeros((P, total), np.float32)
    p = np.arange(P)[:, None]

    def put(name, value):
        c, w = at[name]
        a[:, c:c + w] = value

    head = np.arange(HW)[None, :] // WN
    node = np.arange(HW)[None, :] % WN
    put("ident", p == np.arange(P)[None, :])
    put("before", p < np.arange(P)[None, :])
    put("ones", 1.0)
    put("headmask", np.concatenate([(q * P + p) // F == head for q in range(3)], axis=1))
    hot = p - (ZC - 2 * P)
    outside = np.where((hot >= 0) & (hot < NH) & (hot != node), -BIG, 0.0)
    put("linsel", 1.0 * (p - F == head) - 1.0 * (p - F - H == head) + outside)
    put("hotcols", (p % 3 == 0) & (p < KO) & (p // 3 == np.arange(NH)[None, :]))
    put("nodesel", (p % WN == np.arange(WN)[None, :]) & (p < CN))
    put("winsel", p // WN == np.arange(5)[None, :])
    put("slot", np.where(p <= KX, p // 3, -7))
    put("item_col", p + IP * np.arange(IG)[None, :])
    put("item_row", np.arange(ITEMS)[None, :])
    return a


def build_program(nc, x, src, dst, edge_attr, node_vec1, node_vec1_n2,
                  W1l, b1l, W1r, b1r, att1, bias1, W2l, b2l, W2r, b2r, att2, bias2,
                  Wfc, bfc, ps_w, consts, out):
    Wl, bl, Wr, br = [W1l, W2l], [b1l, b2l], [W1r, W2r], [b1r, b2r]
    att, gat_bias = [att1, att2], [bias1, bias2]
    at, ncols = constant_columns()
    ctx = ExitStack()

    def sb(name, shape, dt=F32):
        return ctx.enter_context(nc.sbuf_tensor(name, shape, dt))

    def sem(name):
        return ctx.enter_context(nc.semaphore(name))

    def dram(name, shape, dt=F32):
        return nc.dram_tensor(name, shape, dt).ap()

    with ctx:
        gat_rows = [dram(f"gat_rows{l}", [N, ROWP]) for l in range(2)]
        dst_rows = [dram(f"dst_rows{l}", [W + 1, KX, ZC], BF16) for l in range(2)]
        feat_rows = dram("feat_rows", [N, F])
        src_tab = dram("src_tab", [RMAX, P, ITEMS], I32)
        relT_tab = dram("relT_tab", [RMAX, ITEMS, P], BF16)
        win_tab = dram("win_tab", [RMAX, ITEMS], I32)

        cst = sb("cst", [P, ncols])

        def const(name, rows=P):
            c, w = at[name]
            return cst[0:rows, c:c + w]

        wl_ext = sb("wl_ext", [F + 1, 2, ROW])
        wr_ext = sb("wr_ext", [F + 1, 2, ZC])
        wl_mix = sb("wl_mix", [P, 2, 3, F])
        wfc_ext = sb("wfc_ext", [F + 1, F])
        att_row = sb("att_row", [P, 2, HF])
        att_col = sb("att_col", [P, 2, 3])
        att_mat = sb("att_mat", [P, 2, 3, HW])
        bias_tmp = sb("bias_tmp", [F + 1, HF])
        lin_tmp = sb("lin_tmp", [F + 1, HF])
        lin_sum = sb("lin_sum", [F + 1, H])
        bl_cols = sb("bl_cols", [F, 2, H])
        bias_col = sb("bias_col", [F, 2])
        out_bias = sb("out_bias", [F, 2])
        ps_row = sb("ps_row", [P, F])
        zero_rows = sb("zero_rows", [KX, ZC], BF16)

        early_a = sb("early_a", [P, 8064])
        early_b = sb("early_b", [P, S * U * ROWP])

        def part(n):
            return early_b[:, n * TC * P:(n + 1) * TC * P].rearrange("p (c e) -> p c e", c=TC)
        src_f, dst_y, win_base = part(0), part(1), part(2)
        src_i, dst_i = part(3).bitcast(I32), part(4).bitcast(I32)
        pick = early_a[:, 0:TC * ITEMS].rearrange("p (c i) -> p c i", c=TC)
        dst_f = sb("dst_f", [P, TC, P + 1])
        ext = sb("ext", [P, 2, TC])
        extw = sb("extw", [P, 2, TC])
        fl_i = sb("fl_i", [P, 2 * TC], I32)
        fl_f = sb("fl_f", [P, 2 * TC])
        fl_r = sb("fl_r", [P, 2 * TC])
        fl_a = sb("fl_a", [P, 2 * TC])
        cnt = sb("cnt", [P, TC])
        cum = sb("cum", [P, TC])
        first = sb("first", [P, TC])
        end = sb("end", [P, TC])
        rounds_f = sb("rounds_f", [P, 1])
        rounds_w = sb("rounds_w", [P, 1])
        rounds_i = sb("rounds_i", [P, 1], I32)
        acc_buf = sb("acc_buf", [P, (W + 1) * (F + 1)])

        def table(n, rows_=P):
            return acc_buf[0:rows_, n * ITEMS:(n + 1) * ITEMS]
        ge, src_o, win_f, win_o = table(0), table(1).bitcast(I32), table(3), table(4, 1).bitcast(I32)
        relT_f = acc_buf[0:IP, 7 * ITEMS:7 * ITEMS + IG * P].rearrange("p (g e) -> p g e", g=IG)
        relT_m = early_b[0:IP, 5 * TC * P:5 * TC * P + IG * P].rearrange("p (g e) -> p g e", g=IG)
        win_c = sb("win_c", [IP, IG])
        relT_o = sb("relT_o", [IP, IG, P], BF16)

        xs = sb("xs", [CN, NC, F])
        xc_buf, xq_buf = sb("xc_buf", [P, NC * F]), sb("xq_buf", [P, NC * F])
        xc = xc_buf[0:CN, :].rearrange("p (c f) -> p c f", f=F)
        xq = xq_buf[0:CN, :].rearrange("p (c f) -> p c f", f=F)
        st = sb("st", [CN, 4, NC])
        cj = sb("cj", [CN, NC])
        ci = sb("ci", [CN, NC])
        h_node = sb("h_node", [CN, F])
        h_T = sb("h_T", [F + 1, UC, CN])
        row_o = early_b[0:CN, 0:UC * ROWP].rearrange("p (u k) -> p u k", u=UC)
        parts = early_b[0:CN, UC * ROWP:UC * ROWP + UC * 3 * ZC // 2].bitcast(BF16).rearrange(
            "p (u s z) -> p u s z", u=UC, s=3)
        rest = sb("rest", [CN, ZC])
        z_loop = sb("z_loop", [CN, ZC])
        s_loop = sb("s_loop", [CN, 2, H])
        d_loop = sb("d_loop", [CN, H, WN])
        inv_l = sb("inv_l", [HW, UC, 5])
        mean_x = sb("mean_x", [HW, 5, 2, F])
        mean_T = sb("mean_T", [P, 5, 3, WN])

        neg_max = sb("neg_max", [HW, W + 1])
        acc = acc_buf[0:HW, :].rearrange("p (w f) -> p w f", f=F + 1)
        acc2 = early_a[0:F, 0:N + SPAN]

        tile_src = sb("tile_src", [P, TROWS], I32)
        tile_rel = sb("tile_rel", [P, TROWS])
        tile_lo = sb("tile_lo", [1, TROWS], I32)
        lo_f = early_b[0:1, 0:TROWS]
        lo_c = sb("lo_c", [P, TC])
        wide = sb("wide", [P, 3])
        rounds2_i = sb("rounds2_i", [P, 1], I32)

        src_s = xc_buf[:, 0:ITEMS].bitcast(I32)
        win_s = sb("win_s", [1, ITEMS], I32)
        idx = sb("idx", [P, S, U], I32)
        rows = early_b[:, :].rearrange("p (s j k) -> p s j k", s=S, j=U)
        n_relu = 2 * 3 * U * P
        relu = early_a[:, 0:n_relu].rearrange("p (b z e) -> p b z e", b=2, z=3)
        dst_w = early_a[0:KO, n_relu:n_relu + S * U * ZE // 2].bitcast(BF16).rearrange(
            "p (s j k) -> p s j k", s=S, j=U)
        rel_b = sb("rel_b", [KO, S, U * P], BF16)
        oh = sb("oh", [KO, 3, U * P], BF16)
        p_T = sb("p_T", [HW, 2, U, P])
        p_e = sb("p_e", [P, U, HW])
        neg_item = sb("neg_item", [HW, 2, U])
        nm = sb("nm", [HW, 2, U])
        dm = sb("dm", [HW, 2, U])
        scale = sb("scale", [HW, 2, U])
        feat_g = sb("feat_g", [P, S, U, F])
        ea = sb("ea", [P, S, U, F])
        pre = sb("pre", [P, 2, U])
        pa = sb("pa", [P, 2, U])
        oh2 = sb("oh2", [P, U, SPAN])
        gate = sb("gate", [P, 2, U, SPAN])

        ps = ctx.enter_context(nc.psum_tensor("ps", [P, 8, 512], F32))

        loaded, phase = sem("loaded"), sem("phase")
        dst_arrived, edges_arrived = sem("dst_arrived"), sem("edges_arrived")
        zeroed = sem("zeroed")
        counted, prefix_done, picked = sem("counted"), sem("prefix_done"), sem("picked")
        expanded, expandedT, tab_ready, tab_stored = (
            sem("expanded"), sem("expandedT"), sem("tab_ready"), sem("tab_stored"))
        var_done, sd_done = sem("var_done"), sem("sd_done")
        zero_stored = sem("zero_stored")
        project_names = ["h_T_done", "proj_r_done", "proj_l_done", "row_done", "hi_done", "rest_done",
                         "r_used", "mid_done", "parts_done", "loop_spread", "loop_turned", "loop_done"]
        mean_names = ["mean_done", "mean_turned", "mean_T_done", "mixed"]
        node_names = [["h_node_done", "h_turned"] + project_names, mean_names + project_names,
                      mean_names + ["h_T_done", "fc_done", "resid_done"]]
        node_sem = [{n: sem(f"{n}{g}") for n in node_names[g]} for g in range(3)]
        node_dma = [[sem(f"node_dma{l}_{u}") for u in range(UC)] for l in range(2)]
        acc_init, tab_loaded = sem("acc_init"), [sem(f"tab_loaded{g}") for g in range(2)]
        tiles_ready, tiles_turned = sem("tiles_ready"), sem("tiles_turned")
        edge_names = ["idx_done", "oh_done", "z_done0", "z_done1", "z_done2", "relu_done0",
                      "relu_done1", "relu_done2", "logit_done0", "logit_done1", "max_done0",
                      "max_done1", "state_done0", "state_done1", "state_done2", "state_done3",
                      "nm_done0", "nm_done1", "p_half_done", "p_done", "scale_done", "p_turned", "p_e_done",
                      "sum_done", "acc_done0", "acc_done1", "acc_done2", "acc_done3"]
        es = {n: sem(n) for n in edge_names}
        gate_names = ["idx2_done", "prod_done", "pre_done", "pa_done", "oh2_done", "gate_done",
                      "sum2_done", "acc2_done0", "acc2_done1", "acc2_done2", "acc2_done3"]
        gs = {n: sem(n) for n in gate_names}
        gathered = [sem(f"gathered{u}") for u in range(S)]
        rel_loaded = [sem(f"rel_loaded{u}") for u in range(S)]
        dst_loaded = [sem(f"dst_loaded{u}") for u in range(S)]
        gathered2 = [sem(f"gathered2_{u}") for u in range(S)]
        ea_loaded = [sem(f"ea_loaded{u}") for u in range(S)]
        held_sp, held_pool, held_pe = sem("held_sp"), sem("held_pool"), sem("held_pe")
        final_done, feat_done, out_stored = sem("final_done"), sem("feat_done"), sem("out_stored")
        feat_stored, sums_turned, sums_taken = sem("feat_stored"), sem("sums_turned"), sem("sums_taken")

        n_loads, n_dst_loads, n_edge_loads = [0], [0], [0]
        held = {}

        def n_rounds(eng):
            return eng.value_load(rounds_i[0:1, 0:1], min_val=1, max_val=RMAX)

        def n_rounds2(eng):
            return eng.value_load(rounds2_i[0:1, 0:1], min_val=1, max_val=-(-N // SPAN))

        def hold(eng, semaphore, value):
            eng.wait_ge(semaphore, value)
            eng.sem_inc(held[eng], 1)

        def barrier(eng, n):
            eng.drain().then_inc(phase, 1)
            eng.wait_ge(phase, 5 * n)

        def logit_bank(u, hh):
            return (3, 4, 7)[(2 * u + hh) % 3]

        def window_regs(eng, engine_type, table, col, top):
            _, regs = nc.values_load_multi_w_load_instructions(
                table[0:1, bass.ds(col, U)], engines=[engine_type], min_val=0, max_val=top,
                skip_runtime_bounds_check_because="phase 1 clamps the tables to these bounds")
            return regs

        def edge_rounds(eng, layer, per_round, body):
            R, nit, before = (n_rounds2(eng), TNIT, 0) if layer == 2 else (n_rounds(eng), NIT, layer)
            with eng.Fori(0, R) as r:
                m_round = eng.snap((r + before * R) * nit + 1)
                per_round(r, eng.snap(m_round * S))

                def at_body(q):
                    m = eng.snap(m_round + q)
                    return q, eng.snap(m * S), m
                body(*at_body(0), True, False)
                with eng.Fori(1, nit - 1) as q:
                    body(*at_body(q), False, False)
                body(*at_body(nit - 1), False, True)

        def l_bank(u):
            return (0, 7)[u % 2]

        def r_bank(u):
            return (1, 2)[u % 2]

        def chunk_bodies(eng, body):
            body(0, 0, True, False)
            with eng.Fori(1, NC // UC - 1) as i:
                body(i, eng.snap(i * UC), False, False)
            body(NC // UC - 1, NC - UC, False, True)

        block = ctx.enter_context(nc.Block())

        @block.sync
        def _(sp):
            held[sp] = held_sp
            def load(dst_ap, src_ap, signal=loaded, count=n_loads):
                count[0] += 16
                with nc.allow_non_contiguous_dma(reason="small weights and columns"):
                    sp.dma_start(dst_ap, src_ap).then_inc(signal, 16)

            sp.wait_ge(zeroed, 1)
            full = (TC - 1) * P * P
            rest_tiles = T - 1 - (TC - 1) * P
            for buf, arr, signal, count in ((dst_i, dst, dst_arrived, n_dst_loads),
                                            (src_i, src, edges_arrived, n_edge_loads)):
                load(buf[:, 0:TC - 1, :], arr[0:full].rearrange("(c p e) -> p c e", c=TC - 1, p=P), signal, count)
                load(buf[0:rest_tiles, TC - 1, :],
                     arr[full:full + rest_tiles * P].rearrange("(p e) -> p e", p=rest_tiles),
                     signal, count)
                seen = (T - 1) * P - LAST
                load(buf[rest_tiles:rest_tiles + 1, TC - 1, seen:P],
                     arr[(T - 1) * P:E].rearrange("(a e) -> a e", a=1), signal, count)
                if arr is dst:
                    load(cst[:, :], consts, edges_arrived, n_edge_loads)
            load(xs[:, :, :], x.rearrange("(c p) f -> p c f", p=CN))
            for l in range(2):
                load(wl_ext[0:F, l, 0:HF], Wl[l])
                load(wr_ext[0:F, l, 0:HF], Wr[l])
                heads = Wl[l].rearrange("f (h k) -> f h k", k=F)
                load(wl_mix[0:F, l, :, :], heads[:, 0:H:2, :])
                load(wl_mix[F:P, l, 0:2, :], heads[:, 1:H:2, :])
                load(wr_ext[F:F + 1, l, 0:HF], bl[l].rearrange("(a k) -> a k", a=1))
                load(att_row[:, l, :], att[l].rearrange("h f -> (h f)").partition_broadcast(P))
                flat = att[l].rearrange("h f -> (h f)")
                for q in range(3):
                    n = min(P, HF - q * P)
                    load(att_col[0:n, l, q:q + 1], flat[q * P:q * P + n].rearrange("(p a) -> p a", a=1))
                load(bl_cols[:, l, :], bl[l].rearrange("(h f) -> f h", f=F))
                load(bias_col[:, l:l + 1], gat_bias[l].rearrange("(p a) -> p a", a=1))
            load(wfc_ext[0:F, :], Wfc)
            load(wfc_ext[F:F + 1, :], bfc.rearrange("(a k) -> a k", a=1))
            load(ps_row[:, :], ps_w.rearrange("a f -> (a f)").partition_broadcast(P))
            load(cj[:, :], node_vec1.rearrange("(c p) a -> p (c a)", p=CN))
            load(ci[:, :], node_vec1_n2.rearrange("(c p) a -> p (c a)", p=CN))
            load(lin_tmp[F:F + 1, :], br[0].rearrange("(a k) -> a k", a=1))
            load(bias_tmp[F:F + 1, :], br[1].rearrange("(a k) -> a k", a=1))
            for l in range(2):
                sp.dma_start(dst_rows[l][W], zero_rows[:, :]).then_inc(zero_stored, 16)
            sp.wait_ge(zero_stored, 32)

            sp.wait_ge(counted, 2)
            R = n_rounds(sp)
            with sp.Fori(0, R) as r:
                hold(sp, tab_ready, r + 1)
                one = bass.ds(r, 1)
                sp.dma_start(src_tab[one].rearrange("a p i -> (a p) i"), src_o[:, :]).then_inc(tab_stored, 16)
                sp.dma_start(win_tab[one], win_o[:, :]).then_inc(tab_stored, 16)
                sp.dma_start(relT_tab[one].rearrange("a (g p) e -> (a p) g e", p=IP),
                             relT_o[:, :, :]).then_inc(tab_stored, 16)
                hold(sp, tab_stored, r * 48 + (48 + 1))
            barrier(sp, 1)

            def load_table(l, r):
                for buf, tab in ((src_s, src_tab), (win_s, win_tab)):
                    ap = tab[bass.ds(r, 1)]
                    sp.dma_start(buf[:, :], ap.rearrange("a p i -> (a p) i") if len(ap.shape) == 3 else ap
                                 ).then_inc(tab_loaded[l], 16)

            def store_projections(l):
                ns = node_sem[l]

                def start_state(i, c):
                    for u in range(UC):
                        hold(sp, node_dma[l][u], (i + 1) * 32)
                    if isinstance(i, int) and i == NC // UC - 1:
                        load_table(l, 0)
                    src_ap = gat_rows[l][bass.ds(c * CN, UC * CN), ZE:ROW].rearrange("(w n) k -> n w k", n=WN)
                    for h in range(H):
                        sp.dma_start(acc[h * WN:(h + 1) * WN, bass.ds(c * 5, UC * 5), :], src_ap
                                     ).then_inc(acc_init, 16)

                def body(i, c, is_first, is_last):
                    for u in range(UC):
                        rows_at = bass.ds((c + u) * CN, CN)
                        hold(sp, ns["row_done"], c + (u + 2))
                        sp.dma_start(gat_rows[l][rows_at, :], row_o[:, u, :]).then_inc(node_dma[l][u], 16)
                        hold(sp, ns["parts_done"], c + (u + 2))
                        sp.dma_start(dst_rows[l].rearrange("w (n s) z -> (w n) s z", s=3)[rows_at],
                                     parts[:, u, :, :]).then_inc(node_dma[l][u], 16)
                        if u == 1 and not is_first:
                            start_state(i - 1, c - UC)
                    if is_last:
                        start_state(i, c)
                chunk_bodies(sp, body)

            def edges(l):
                def per_round(r, k):
                    hold(sp, es["acc_done3"], k)
                    with sp.If(r > 0):
                        load_table(l, r)
                    hold(sp, tab_loaded[l], (r + 1) * 32)
                    cur[0] = r

                def body(q, k, m, is_first, is_last):
                    for u in range(S):
                        col = q * ITER + u * U
                        wins = window_regs(sp, mybir.EngineType.SP, win_s, col, W)
                        hold(sp, es["oh_done"], k + (u - S + 1))
                        sp.dma_start(rel_b[:, u, :],
                                     relT_tab[bass.ds(cur[0], 1), bass.ds(col, U), :].rearrange(
                                         "a i e -> (a i e)").partition_broadcast(KO)
                                     ).then_inc(rel_loaded[u], 16)
                        hold(sp, es["z_done2"], k + (u - S + 1))
                        for j in range(U):
                            sp.dma_start(dst_w[0:KX, u, j, 0:ZC],
                                         dst_rows[l][bass.ds(wins[j], 1)].rearrange("a k z -> (a k) z")
                                         ).then_inc(dst_loaded[u], 16)
                cur = [0]
                edge_rounds(sp, l, per_round, body)

            for l in range(2):
                store_projections(l)
                barrier(sp, 2 + 2 * l)
                edges(l)
                barrier(sp, 3 + 2 * l)
            with sp.Fori(0, NC // UC) as i:
                hold(sp, feat_done, i + 1)
                group = bass.ds(i * UC, UC)
                sp.dma_start(feat_rows.rearrange("(c p) f -> p c f", p=CN)[:, group, :], xq[:, group, :]
                             ).then_inc(feat_stored, 16)
            sp.wait_ge(feat_stored, 16 * (NC // UC))
            barrier(sp, 6)

            def body2(q, k, m, is_first, is_last):
                for u in range(S):
                    hold(sp, gs["pre_done"], k + (u - S + 1))
                    for j in range(U):
                        at_tile = u * U + j
                        e0 = min((q * ITER + at_tile) * P, LAST) if is_last else q * (ITER * P) + at_tile * P
                        sp.dma_start(ea[:, u, j, :], edge_attr[bass.ds(e0, P), :]).then_inc(ea_loaded[u], 16)
            edge_rounds(sp, 2, lambda r, k: None, body2)
            sp.wait_ge(final_done, 1)
            sp.dma_start(out.rearrange("(c p) f -> p c f", p=CN), xs[:, :, :]).then_inc(out_stored, 16)
            sp.wait_ge(out_stored, 16)

        @block.gpsimd
        def _(pool):
            held[pool] = held_pool
            for s in list(es.values()) + list(gs.values()):
                pool.sem_inc(s, S)
            for ns in node_sem:
                for s in ns.values():
                    pool.sem_inc(s, 1)
            pool.sem_inc(tab_stored, 1)
            pool.wait_ge(counted, 2)
            barrier(pool, 1)
            pool.memset(dst_w[:, :, :, :], 0.0)
            pool.drain()
            pool.tensor_copy(dst_w.rearrange("p s j k -> p (s j) k")[:, :, ZC:ZE],
                             const("hotcols", KO).unsqueeze(1).to_broadcast([KO, S * U, NH]))

            def gathers(target, table, width, sems, done, used):
                def body(q, k, m, is_first, is_last):
                    for u in range(S):
                        pool.wait_ge(used, k + (u - S + 1))
                        hold(pool, done, k + (u + 1))
                        for j in range(U):
                            pool.indirect_dma_start(
                                out=target[:, u, j, :], out_offset=None, in_=table,
                                in_offset=bass.IndirectOffsetOnAxis(ap=idx[:, u, j:j + 1], axis=0)
                            ).then_inc(sems[u], 16)
                return body
            for l in range(2):
                barrier(pool, 2 + 2 * l)
                edge_rounds(pool, l, lambda r, k: None,
                            gathers(rows, gat_rows[l][:, :], ROWP, gathered, es["idx_done"], es["sum_done"]))
                barrier(pool, 3 + 2 * l)
            barrier(pool, 6)
            edge_rounds(pool, 2, lambda r, k: None,
                        gathers(feat_g, feat_rows[:, :], F, gathered2, gs["idx2_done"], gs["sum2_done"]))

        @block.scalar
        def _(act):
            def root(order, c, n):
                act.wait_ge(var_done, order)
                act.activation(st[:, 2, bass.ds(c, n)], st[:, 1, bass.ds(c, n)], ACT.Sqrt).then_inc(sd_done, 1)

            root(1, 0, NC)
            act.wait_ge(counted, 2)
            barrier(act, 1)

            def node_stage(g):
                ns = node_sem[g]

                def turn_h(c, u):
                    act.wait_ge(ns["h_turned"], c + (u + 2))
                    act.activation(h_T[0:F, u % UC, :], ps[0:F, 6, 0:CN], ACT.Copy).then_inc(ns["h_T_done"], 1)

                def turn_mean(c, u):
                    act.wait_ge(ns["mean_turned"], c + (u + 2))
                    act.wait_ge(ns["mixed"], c + (u + 1))
                    for v, n in ((0, 4), (4, 1)):
                        turned = ps[:, 4 + v // 4, 0:n * HW].rearrange("p (v h n) -> p v h n", v=n, h=H)
                        act.activation(mean_T[0:F, v:v + n, :, :], turned[0:F, :, 0:H:2, :], ACT.Copy)
                        i = act.activation(mean_T[F:P, v:v + n, 0:2, :], turned[F:P, :, 1:H:2, :], ACT.Copy)
                    i.then_inc(ns["mean_T_done"], 1)

                def finish_layer(c, u):
                    act.wait_ge(ns["mixed"], c + (u + 2))
                    act.activation(h_T[0:F, u % UC, :], ps[0:F, 6, 0:CN], ACT.Relu, bias=out_bias[:, g - 1:g],
                                   scale=1.0 / H).then_inc(ns["h_T_done"], 1)

                def projections(i, c, u):
                    if not (isinstance(i, int) and i == 0):
                        act.wait_ge(node_dma[g][u], i * 32)
                    act.wait_ge(ns["proj_r_done"], c + (u + 2))
                    act.activation(parts[:, u, 0, :], ps[0:CN, r_bank(u), 0:ZC], ACT.Copy).then_inc(ns["hi_done"], 1)
                    act.wait_ge(ns["proj_l_done"], c + (u + 2))
                    act.activation(row_o[:, u, 0:ROW], ps[0:CN, l_bank(u), 0:ROW], ACT.Copy).then_inc(ns["row_done"], 1)
                    act.wait_ge(ns["rest_done"], c + (u + 2))
                    act.activation(parts[:, u, 1, :], rest[:, :], ACT.Copy).then_inc(ns["mid_done"], 1)

                def body(i, c, is_first, is_last):
                    for u in range(UC):
                        more = not (is_last and u == UC - 1)
                        if more:
                            (turn_mean if g > 0 else turn_h)(c, u + 1)
                        if g < 2:
                            projections(i, c, u)
                        if g > 0 and more:
                            finish_layer(c, u + 1)
                        if g == 2 and u == 2 and not is_first:
                            root(i + 1, c - UC, UC)
                if g > 0:
                    turn_mean(0, 0)
                    finish_layer(0, 0)
                else:
                    turn_h(0, 0)
                chunk_bodies(act, body)
                if g == 2:
                    root(NC // UC + 1, NC - UC, UC)

            def edges(l):
                def make_idx(k, u, table_col):
                    act.wait_ge(es["sum_done"], k + (u - S + 1))
                    act.copy(idx[:, u % S, :], src_s[:, bass.ds(table_col, U)]).then_inc(es["idx_done"], 1)

                def per_round(r, k):
                    act.wait_ge(tab_loaded[l], (r + 1) * 32)
                    for u in range(AHEAD):
                        make_idx(k, u, u * U)

                def exps(k, u, hh):
                    b = u % 2
                    act.wait_ge(es[f"nm_done{hh}"], k + (u + 1))
                    act.wait_ge(es["p_turned"], k + (u - 1))
                    for j in (2 * hh, 2 * hh + 1):
                        logit = ps[0:HW, logit_bank(u, hh), (j % 2) * P:(j % 2 + 1) * P]
                        i = act.activation(p_T[:, b, j, :], logit, ACT.Exp, bias=nm[:, b, j:j + 1])
                    if hh == 0:
                        i.then_inc(es["p_half_done"], 1)
                    else:
                        i.then_inc(es["p_done"], 1)
                        act.wait_ge(es["acc_done3"], k + (u - 1))
                        act.activation(scale[:, b, :], dm[:, b, :], ACT.Exp).then_inc(es["scale_done"], 1)

                def copy_p(k, u):
                    act.wait_ge(es["p_turned"], k + (u + 1))
                    act.wait_ge(es["sum_done"], k + u)
                    act.copy(p_e[:, :, :].rearrange("p j k -> p (j k)"), ps[:, 5, 0:U * HW]
                             ).then_inc(es["p_e_done"], 1)

                def body(q, k, m, is_first, is_last):
                    for u in range(S + 2 if is_last else S):
                        b = u % 2
                        if u < S:
                            act.wait_ge(es["logit_done1"], k + (u - 1))
                            for z in range(2):
                                act.wait_ge(es[f"z_done{z}"], k + (u + 1))
                                act.activation(relu[:, b, z, :], ps[:, z, :], ACT.Relu
                                               ).then_inc(es[f"relu_done{z}"], 1)
                        if not (is_first and u < 2):
                            exps(k, u - 2, 1)
                            copy_p(k, u - 2)
                        if not (is_first and u < 1) and u <= S:
                            exps(k, u - 1, 0)
                        if not (is_last and u + AHEAD >= S):
                            make_idx(k, u + AHEAD, q * ITER + (u + AHEAD) * U)
                edge_rounds(act, l, per_round, body)

            for l in range(2):
                node_stage(l)
                barrier(act, 2 + 2 * l)
                edges(l)
                barrier(act, 3 + 2 * l)
            node_stage(2)
            barrier(act, 6)

            def make_idx2(k, u, table_col):
                act.wait_ge(gs["sum2_done"], k + (u - S + 1))
                act.copy(idx[:, u % S, :], tile_src[:, bass.ds(table_col, U)]).then_inc(gs["idx2_done"], 1)

            def per_round2(r, k):
                for u in range(AHEAD):
                    make_idx2(k, u, u * U)

            def body2(q, k, m, is_first, is_last):
                for u in range(S):
                    act.wait_ge(gs["pre_done"], k + (u + 1))
                    act.wait_ge(gs["gate_done"], k + (u - 1))
                    act.activation(pa[:, u % 2, :], pre[:, u % 2, :], ACT.Sigmoid).then_inc(gs["pa_done"], 1)
                    if not (is_last and u + AHEAD >= S):
                        make_idx2(k, u + AHEAD, q * ITER + (u + AHEAD) * U)
            edge_rounds(act, 2, per_round2, body2)

        @block.tensor
        def _(pe):
            held[pe] = held_pe
            mm = pe.matmul
            ident = const("ident")

            def turn(o, i, rows_, start=True, stop=True):
                return mm(o, i, cst[0:rows_, at["ident"][0]:at["ident"][0] + rows_], start=start, stop=stop,
                          is_transpose=True)

            pe.wait_ge(counted, 1)
            mm(ps[:, 0, 0:TC], const("before"), cnt[:, :], start=True, stop=False)
            mm(ps[:, 0, 0:TC], const("ones"), fl_f[:, 0:TC], start=False, stop=True)
            mm(ps[:, 1, 0:1], const("ones"), cum[:, TC - 1:TC], start=True, stop=True).then_inc(prefix_done, 1)
            pe.wait_ge(counted, 2)
            R = n_rounds(pe)
            with pe.Fori(0, R) as r:
                for t in range(TC):
                    pe.wait_ge(picked, r * TC + (t + 1))
                    for a, lhs in enumerate((src_f[:, t, :], win_base[:, t, :])):
                        for hh in range(2):
                            m = mm(ps[:, 2 * a + hh, 0:HALF], lhs,
                                   pick[:, t, hh * HALF:(hh + 1) * HALF], start=(t == 0), stop=(t == TC - 1))
                m.then_inc(expanded, 1)
                for g in range(IG):
                    for t in range(TC):
                        m = mm(ps[0:IP, 4 + g // 3, (g % 3) * (P + 1):(g % 3 + 1) * (P + 1)],
                               pick[:, t, g * IP:(g + 1) * IP], dst_f[:, t, :], start=(t == 0), stop=(t == TC - 1))
                m.then_inc(expandedT, 1)
            pe.wait_ge(tiles_ready, 1)
            for t in range(TC):
                for a, i in enumerate((src_f[:, t, :], dst_f[:, t, 0:P], lo_c[:, t:t + 1].to_broadcast([P, P]))):
                    turn(ps[:, 2 * a + t // 4, (t % 4) * P:(t % 4 + 1) * P], i, P)
            turn(ps[:, 6, 0:P], wide[:, 0:1].to_broadcast([P, P]), P).then_inc(tiles_turned, 1)
            barrier(pe, 1)

            def node_stage(g):
                ns = node_sem[g]

                def turn_h(c, u):
                    pe.wait_ge(ns["h_node_done"], c + (u + 2))
                    hold(pe, ns["h_T_done"], c + (u + 1))
                    turn(ps[0:F, 6, 0:CN], h_node[:, :], CN).then_inc(ns["h_turned"], 1)

                def turn_mean(c, u):
                    pe.wait_ge(ns["mean_done"], c + (u + 2))
                    hold(pe, ns["mean_T_done"], c + (u + 1))
                    for v in range(5):
                        m = turn(ps[:, 4 + v // 4, (v % 4) * HW:(v % 4 + 1) * HW],
                                 mean_x[:, v, :, :].rearrange("p a f -> p (a f)"), HW)
                    m.then_inc(ns["mean_turned"], 1)

                def mix(c, u):
                    pe.wait_ge(ns["mean_T_done"], c + (u + 2))
                    hold(pe, ns["h_T_done"], c + (u + 1))
                    for a in range(3):
                        rows_ = P if a < 2 else F
                        m = mm(ps[0:F, 6, 0:CN], wl_mix[0:rows_, g - 1, a, :],
                               mean_T[0:rows_, :, a, :], start=(a == 0), stop=(a == 2))
                    m.then_inc(ns["mixed"], 1)

                def project(c, u):
                    pe.wait_ge(ns["h_T_done"], c + (u + 2))
                    ago = 1 if u == 0 else 2
                    pe.wait_ge(ns["row_done"], c + (u + 2 - ago))
                    pe.wait_ge(ns["r_used"], c + (u + 2 - ago))
                    mm(ps[0:CN, r_bank(u), 0:ZC], h_T[:, u, :], wr_ext[:, g, :], start=True, stop=True
                       ).then_inc(ns["proj_r_done"], 1)
                    mm(ps[0:CN, l_bank(u), 0:ROW], h_T[:, u, :], wl_ext[:, g, :], start=True, stop=True
                       ).then_inc(ns["proj_l_done"], 1)

                def spread_loops(c, u):
                    pe.wait_ge(ns["loop_spread"], c + (u + 2))
                    pe.wait_ge(ns["loop_done"], c + (u + 1))
                    mm(ps[0:HW, 3, 0:5], d_loop[:, :, :].rearrange("p h n -> p (h n)"), const("winsel", CN),
                       start=True, stop=True).then_inc(ns["loop_turned"], 1)

                def final_linear(c, u):
                    pe.wait_ge(ns["h_T_done"], c + (u + 2))
                    pe.wait_ge(ns["resid_done"], c + (u + 1))
                    mm(ps[0:CN, 7, 0:F], h_T[:, u, :], wfc_ext[:, :], start=True, stop=True
                       ).then_inc(ns["fc_done"], 1)

                def body(i, c, is_first, is_last):
                    for u in range(UC):
                        more = not (is_last and u == UC - 1)
                        if more:
                            (turn_mean if g > 0 else turn_h)(c, u + 1)
                        if g == 2:
                            final_linear(c, u)
                        else:
                            project(c, u)
                            if not (is_first and u == 0):
                                spread_loops(c, u - 1)
                        if g > 0 and more:
                            mix(c, u + 1)
                    if g < 2 and is_last:
                        spread_loops(c, UC - 1)
                if g > 0:
                    turn_mean(0, 0)
                    mix(0, 0)
                else:
                    turn_h(0, 0)
                chunk_bodies(pe, body)

            def edges(l):
                def z_step(k, m_, u):
                    pe.wait_ge(gathered[u], m_ * (16 * U))
                    pe.wait_ge(dst_loaded[u], m_ * (16 * U))
                    pe.wait_ge(es["oh_done"], k + (u + 1))
                    for z in range(3):
                        n = ZQ[z]
                        pe.wait_ge(es[f"relu_done{z}"], k + u)
                        for j in range(U):
                            o = ps[0:n, z, j * P:(j + 1) * P]
                            turn(o, rows[:, u, j, z * P:z * P + n], P, stop=False)
                            m = mm(o, dst_w[:, u, j, z * P:z * P + n], oh[:, u % 3, j * P:(j + 1) * P],
                                   start=False, stop=True)
                        m.then_inc(es[f"z_done{z}"], 1)

                def logits(k, u, hh):
                    b = u % 2
                    if hh == 0:
                        for z in range(3):
                            pe.wait_ge(es[f"relu_done{z}"], k + (u + 1))
                        pe.wait_ge(es["p_done"], k + (u - 1))
                    else:
                        pe.wait_ge(es["p_half_done"], k + u)
                    cols = slice(hh * 2 * P, (hh + 1) * 2 * P)
                    o = ps[0:HW, logit_bank(u, hh), 0:2 * P]
                    for z in range(3):
                        n = ZQ[z]
                        m = mm(o, att_mat[0:n, l, z, :], relu[0:n, b, z, cols], start=(z == 0), stop=(z == 2))
                    m.then_inc(es[f"logit_done{hh}"], 1)

                def turn_p(k, u):
                    pe.wait_ge(es["p_done"], k + (u + 1))
                    pe.wait_ge(es["p_e_done"], k + u)
                    for j in range(U):
                        m = turn(ps[:, 5, j * HW:(j + 1) * HW], p_T[:, u % 2, j, :], HW)
                    m.then_inc(es["p_turned"], 1)

                def sums(k, u):
                    pe.wait_ge(es["p_e_done"], k + (u + 1))
                    pe.wait_ge(es["acc_done3"], k + u)
                    for j in range(U):
                        m = mm(ps[0:HW, 6, j * (F + 1):(j + 1) * (F + 1)], p_e[:, j, :],
                               rows[:, u % S, j, ZE:ROW], start=True, stop=True)
                    m.then_inc(es["sum_done"], 1)

                def body(q, k, m, is_first, is_last):
                    for u in range(S + 2 if is_last else S):
                        lag1 = not (is_first and u < 1) and u <= S
                        lag2 = not (is_first and u < 2)
                        if u < S:
                            z_step(k, m, u)
                        if lag1:
                            logits(k, u - 1, 0)
                        if lag2:
                            turn_p(k, u - 2)
                        if lag1:
                            logits(k, u - 1, 1)
                        if lag2:
                            sums(k, u - 2)
                edge_rounds(pe, l, lambda r, k: None, body)

            for l in range(2):
                node_stage(l)
                barrier(pe, 2 + 2 * l)
                edges(l)
                barrier(pe, 3 + 2 * l)
            node_stage(2)
            barrier(pe, 6)

            def body2(q, k, m, is_first, is_last):
                for u in range(S):
                    b = u % 2
                    pe.wait_ge(gathered2[u], m * (16 * U))
                    pe.wait_ge(gs["gate_done"], k + (u + 1))
                    pe.wait_ge(gs["acc2_done3"], k + (u - 1))
                    for j in range(U):
                        i = mm(ps[0:F, b, j * SPAN:(j + 1) * SPAN], feat_g[:, u, j, :], gate[:, b, j, :],
                               start=True, stop=True)
                    i.then_inc(gs["sum2_done"], 1)
            edge_rounds(pe, 2, lambda r, k: None, body2)
            pe.wait_ge(sums_taken, 1)
            for c in range(NC):
                i = turn(ps[0:CN, c // 8, (c % 8) * F:(c % 8 + 1) * F], acc2[:, c * CN:(c + 1) * CN], F)
            i.then_inc(sums_turned, 1)

        @block.vector
        def _(dve):
            TT, TS, STT, CP = dve.tensor_tensor, dve.tensor_scalar, dve.scalar_tensor_tensor, dve.tensor_copy

            def settle():
                dve.drain()

            dve.memset(src_i[:, TC - 1, :], 0)
            dve.memset(dst_i[:, TC - 1, :], -1)
            dve.memset(zero_rows[:, :], 0.0)
            dve.memset(wl_ext[:, :, :], 0.0)
            dve.memset(att_col[:, :, :], 0.0)
            dve.memset(h_T[:, :, :], 1.0)
            dve.memset(neg_max[:, :], 0.0)
            settle()
            dve.memset(cum[:, :], 1.0).then_inc(zeroed, 1)
            dve.wait_ge(dst_arrived, n_dst_loads[0])

            CP(dst_f[:, :, 0:P], dst_i[:, :, :])
            settle()
            TS(dst_y[:, :, :], dst_f[:, :, 0:P], 0.0, 1.0e6, ALU.is_lt, ALU.mult)
            dve.tensor_reduce(ext[:, 1, :], dst_f[:, :, 0:P], AX.X, ALU.max)
            settle()
            TT(dst_y[:, :, :], dst_y[:, :, :], dst_f[:, :, 0:P], ALU.add)
            settle()
            dve.tensor_reduce(ext[:, 0, :], dst_y[:, :, :], AX.X, ALU.min)
            settle()

            def floor_div(o, a, d, n):
                TS(fl_i[:, 0:n], a, 1.0 / d, None, ALU.mult)
                settle()
                CP(fl_f[:, 0:n], fl_i[:, 0:n])
                settle()
                STT(fl_r[:, 0:n], fl_f[:, 0:n], -float(d), a, ALU.mult, ALU.add)
                settle()
                TS(fl_a[:, 0:n], fl_r[:, 0:n], float(d), None, ALU.is_ge)
                TS(fl_r[:, 0:n], fl_r[:, 0:n], 0.0, None, ALU.is_lt)
                settle()
                TT(fl_a[:, 0:n], fl_a[:, 0:n], fl_r[:, 0:n], ALU.subtract)
                settle()
                TT(o, fl_a[:, 0:n], fl_f[:, 0:n], ALU.add)
                settle()

            floor_div(extw[:, :, :].rearrange("p a c -> p (a c)"), ext[:, :, :].rearrange("p a c -> p (a c)"),
                      WN, 2 * TC)
            TT(cnt[:, :], extw[:, 1, :], extw[:, 0, :], ALU.subtract)
            settle()
            TS(cnt[:, :], cnt[:, :], 1.0, 0.0, ALU.add, ALU.max)
            settle()
            dve.wait_ge(edges_arrived, n_edge_loads[0])
            dve.tensor_tensor_scan(cum[:, :], cst[:, at["ones"][0]:at["ones"][0] + TC], cnt[:, :], 0.0,
                                   ALU.mult, ALU.add)
            settle()
            TT(fl_f[:, 0:TC], cum[:, :], cnt[:, :], ALU.subtract)
            settle()
            dve.memset(fl_r[:, :], 0.0).then_inc(counted, 1)
            dve.wait_ge(prefix_done, 1)
            CP(first[:, :], ps[:, 0, 0:TC])
            CP(src_f[:, :, :], src_i[:, :, :])
            TS(rounds_f[:, :], ps[:, 1, 0:1], float(ITEMS - 1), None, ALU.add)
            settle()
            TT(end[:, :], first[:, :], cnt[:, :], ALU.add)
            TT(dst_f[:, :, P], extw[:, 0, :], first[:, :], ALU.subtract)
            floor_div(rounds_w[:, :], rounds_f[:, :], ITEMS, 1)
            CP(rounds_i[:, :], rounds_w[:, :])
            settle()
            dve.memset(fl_r[:, :], 0.0).then_inc(counted, 1)

            def prepare_weights():
                TT(wr_ext[F:F + 1, 0, 0:HF], wr_ext[F:F + 1, 0, 0:HF], lin_tmp[F:F + 1, :], ALU.add)
                TT(wr_ext[F:F + 1, 1, 0:HF], wr_ext[F:F + 1, 1, 0:HF], bias_tmp[F:F + 1, :], ALU.add)
                for l in range(2):
                    CP(wl_ext[:, l, ZE:ROW], cst[0:F + 1, at["ident"][0]:at["ident"][0] + F + 1])
                    dve.tensor_reduce(out_bias[:, l:l + 1], bl_cols[:, l, :], AX.X, ALU.add)
                    for z in range(3):
                        TS(att_mat[:, l, z, :], cst[:, at["headmask"][0] + z * HW:at["headmask"][0] + (z + 1) * HW],
                           att_col[:, l, z:z + 1], 0.8, ALU.mult, ALU.mult)
                settle()
                for l in range(2):
                    TT(att_mat[:, l, 2, :], att_mat[:, l, 2, :], const("linsel"), ALU.add)
                    STT(out_bias[:, l:l + 1], out_bias[:, l:l + 1], 1.0 / H, bias_col[:, l:l + 1], ALU.mult, ALU.add)
                    for w_ext in (wl_ext, wr_ext):
                        TT(lin_tmp[:, :], w_ext[:, l, 0:HF], att_row[0:F + 1, l, :], ALU.mult)
                        settle()
                        dve.tensor_reduce(lin_sum[:, :], lin_tmp[:, :].rearrange("p (h f) -> p h f", h=H), AX.X, ALU.add)
                        settle()
                        TS(w_ext[:, l, HF:HF + H], lin_sum[:, :], 0.2, None, ALU.mult)
                        TS(w_ext[:, l, HF + H:ZC], lin_sum[:, :], -0.2, None, ALU.mult)
                        settle()

            def center(c, n):
                xg, st0 = xs[:, bass.ds(c, n), :], st[:, 0, bass.ds(c, n)]
                dve.tensor_reduce(st0, xg, AX.X, ALU.add)
                settle()
                TS(st0, st0, 1.0 / F, None, ALU.mult)
                settle()
                TT(xc[:, bass.ds(c, n), :], xg, st0.unsqueeze(2).to_broadcast([CN, n, F]), ALU.subtract)
                settle()

            def variance(c, n):
                xg, xqg, st0 = xc[:, bass.ds(c, n), :], xq[:, bass.ds(c, n), :], st[:, 0, bass.ds(c, n)]
                TT(xqg, xg, xg, ALU.mult)
                settle()
                dve.tensor_reduce(st0, xqg, AX.X, ALU.add)
                settle()
                TS(st[:, 1, bass.ds(c, n)], st0, 1.0 / F, EPS, ALU.mult, ALU.add).then_inc(var_done, 1)

            R = n_rounds(dve)
            with dve.Fori(0, R) as r:
                dve.wait_ge(tab_stored, r * 48 + 1)
                CP(win_base[:, :, :], dst_f[:, :, P:P + 1].to_broadcast([P, TC, P]))
                settle()
                for t in range(TC):
                    TS(ge[:, :], const("item_row"), first[:, t:t + 1], None, ALU.is_ge)
                    settle()
                    STT(pick[:, t, :], const("item_row"), end[:, t:t + 1], ge[:, :], ALU.is_lt, ALU.mult
                        ).then_inc(picked, 1)
                    settle()
                with dve.If(r < 1):
                    dve.wait_ge(loaded, n_loads[0])
                    prepare_weights()
                    center(0, NC)
                    variance(0, NC)
                    dve.wait_ge(sd_done, 1)
                    dve.reciprocal(st[:, 3, :], st[:, 2, :])
                    settle()
                dve.wait_ge(expanded, r + 1)

                def halves(a, n=P):
                    return ps[0:n, 2 * a:2 * a + 2, 0:HALF]

                def two(ap):
                    return ap.rearrange("p (a b) -> p a b", a=2)
                CP(two(src_o[:, :]), halves(0))
                TT(two(win_f[:, :]), halves(1), two(const("item_row")), ALU.add)
                settle()
                TS(win_f[:, :], win_f[:, :], float(W), None, ALU.min)
                settle()
                CP(win_o[:, :], win_f[0:1, :])
                settle()
                dve.wait_ge(expandedT, r + 1)
                for g in range(IG):
                    o = ps[0:IP, 4 + g // 3, (g % 3) * (P + 1):(g % 3 + 1) * (P + 1)]
                    TT(win_c[:, g:g + 1], o[:, P:P + 1], const("item_col", IP)[:, g:g + 1], ALU.add)
                settle()
                TS(win_c[:, :], win_c[:, :], float(W), -float(WN), ALU.min, ALU.mult)
                settle()
                for g in range(IG):
                    o = ps[0:IP, 4 + g // 3, (g % 3) * (P + 1):(g % 3 + 1) * (P + 1)]
                    TS(relT_f[:, g, :], o[:, 0:P], win_c[:, g:g + 1], None, ALU.add)
                settle()
                TS(relT_m[:, :, :], relT_f[:, :, :], 0.0, None, ALU.is_ge)
                settle()
                STT(relT_m[:, :, :], relT_f[:, :, :], float(WN - 1), relT_m[:, :, :], ALU.is_le, ALU.mult)
                settle()
                STT(relT_f[:, :, :], relT_f[:, :, :], float(WN), relT_m[:, :, :], ALU.subtract, ALU.mult)
                settle()
                TS(relT_o[:, :, :], relT_f[:, :, :], float(WN), None, ALU.add)
                TS(first[:, :], first[:, :], -float(ITEMS), None, ALU.add)
                TS(end[:, :], end[:, :], -float(ITEMS), None, ALU.add)
                TS(dst_f[:, :, P], dst_f[:, :, P], float(ITEMS), None, ALU.add)
                settle()
                dve.memset(fl_r[:, :], 0.0).then_inc(tab_ready, 1)

            TS(lo_c[:, :], ext[:, 0, :], float(N), None, ALU.min)
            TT(cnt[:, :], ext[:, 1, :], ext[:, 0, :], ALU.subtract)
            settle()
            dve.tensor_reduce(wide[:, 0:1], cnt[:, :], AX.X, ALU.max).then_inc(tiles_ready, 1)
            dve.wait_ge(tiles_turned, 1)

            def cols(ap):
                return ap[:, 0:4 * P], ap[:, 4 * P:TROWS]
            for o, src_p, lo_p in zip(range(2), (ps[:, 0, :], ps[:, 1, 0:TROWS - 4 * P]),
                                      (ps[:, 4, :], ps[:, 5, 0:TROWS - 4 * P])):
                CP(cols(tile_src)[o], src_p)
                CP(cols(tile_lo)[o], lo_p[0:1, :])
                CP(cols(tile_rel)[o], lo_p)
            dve.tensor_reduce(wide[:, 1:2], ps[:, 6, 0:P], AX.X, ALU.max)
            settle()
            for o, dst_p in zip(range(2), (ps[:, 2, :], ps[:, 3, 0:TROWS - 4 * P])):
                TT(cols(tile_rel)[o], dst_p, cols(tile_rel)[o], ALU.subtract)
            floor_div(wide[:, 2:3], wide[:, 1:2], SPAN, 1)
            TS(wide[:, 2:3], wide[:, 2:3], 1.0, None, ALU.add)
            settle()
            CP(rounds2_i[:, :], wide[:, 2:3])
            settle()

            barrier(dve, 1)
            dve.memset(row_o[:, :, ROW:ROWP], 0.0)
            dve.memset(acc[:, W, :], 1.0)
            settle()

            def node_stage(g):
                ns = node_sem[g]

                def h_of(c, u):
                    dve.wait_ge(ns["h_turned"], c + (u + 1))
                    TS(h_node[:, :], xc[:, bass.ds(c + u, 1), :].rearrange("p a f -> p (a f)"),
                       st[:, 3, bass.ds(c + u, 1)], 0.0, ALU.mult, ALU.max).then_inc(ns["h_node_done"], 1)

                def mean(c, u):
                    a = acc[:, bass.ds((c + u) * 5, 5), :]
                    dve.reciprocal(inv_l[:, u % UC, :], a[:, :, F])
                    settle()
                    dve.wait_ge(ns["mean_turned"], c + (u + 1))
                    TT(mean_x[:, :, :, :], a[:, :, 0:F].unsqueeze(2).to_broadcast([HW, 5, 2, F]),
                       inv_l[:, u % UC, :].unsqueeze(2).unsqueeze(3).to_broadcast([HW, 5, 2, F]), ALU.mult
                       ).then_inc(ns["mean_done"], 1)

                def take_loops(c, u):
                    dve.wait_ge(ns["loop_turned"], c + (u + 2))
                    TS(neg_max[:, bass.ds((c + u) * 5, 5)], ps[0:HW, 3, 0:5], -1.0, None, ALU.mult
                       ).then_inc(ns["loop_done"], 1)

                def project(c, u, lag):
                    r_ps = ps[0:CN, r_bank(u), 0:ZC]
                    dve.wait_ge(ns["hi_done"], c + (u + 2))
                    TT(rest[:, :], r_ps, parts[:, u, 0, :], ALU.subtract).then_inc(ns["rest_done"], 1)
                    dve.wait_ge(ns["row_done"], c + (u + 2))
                    TT(z_loop[:, :], r_ps, row_o[:, u, 0:ZC], ALU.add).then_inc(ns["r_used"], 1)
                    settle()
                    STT(z_loop[:, 0:HF], z_loop[:, 0:HF], 0.0, att_row[0:CN, g, :], ALU.max, ALU.mult)
                    settle()
                    dve.tensor_reduce(s_loop[:, 0, :], z_loop[:, 0:HF].rearrange("p (h f) -> p h f", h=H), AX.X, ALU.add)
                    if lag:
                        take_loops(c, u - 1)
                    settle()
                    STT(s_loop[:, 1, :], s_loop[:, 0, :], 0.8, z_loop[:, HF:HF + H], ALU.mult, ALU.add)
                    dve.wait_ge(ns["mid_done"], c + (u + 2))
                    TT(parts[:, u, 2, :], rest[:, :], parts[:, u, 1, :], ALU.subtract).then_inc(ns["parts_done"], 1)
                    settle()
                    dve.wait_ge(ns["loop_turned"], c + (u + 1))
                    TT(d_loop[:, :, :], s_loop[:, 1, :].unsqueeze(2).to_broadcast([CN, H, WN]),
                       const("nodesel", CN).unsqueeze(1).to_broadcast([CN, H, WN]), ALU.mult
                       ).then_inc(ns["loop_spread"], 1)

                def add_linear(c, u):
                    dve.wait_ge(ns["fc_done"], c + (u + 2))
                    xr = xs[:, bass.ds(c + u, 1), :].rearrange("p a f -> p (a f)")
                    TT(xr, xr, ps[0:CN, 7, 0:F], ALU.add).then_inc(ns["resid_done"], 1)

                def features(i, c, step):
                    group = bass.ds(c, UC)
                    if step == 0:
                        settle()
                        center(c, UC)
                    elif step == 1:
                        variance(c, UC)
                    elif step == 3:
                        dve.wait_ge(sd_done, i + 2)
                        dve.reciprocal(st[:, 3, group], st[:, 2, group])
                        settle()
                        TT(xq[:, group, :], xc[:, group, :], st[:, 3, group].unsqueeze(2).to_broadcast([CN, UC, F]), ALU.mult)
                        settle()
                    elif step == 4:
                        TS(xq[:, group, :], xq[:, group, :], 0.0, None, ALU.max)
                        settle()
                        TT(xq[:, group, :], xq[:, group, :], cj[:, group].unsqueeze(2).to_broadcast([CN, UC, F]), ALU.mult
                           ).then_inc(feat_done, 1)

                def body(i, c, is_first, is_last):
                    for u in range(UC):
                        if not (is_last and u + 2 >= UC):
                            (mean if g > 0 else h_of)(c, u + 2)
                        if g == 2:
                            add_linear(c, u)
                            if not is_first:
                                features(i - 1, c - UC, u)
                        else:
                            project(c, u, not (is_first and u == 0))
                    if g < 2 and is_last:
                        take_loops(c, UC - 1)
                for u in range(2):
                    (mean if g > 0 else h_of)(0, u)
                if g == 2:
                    dve.memset(acc2[:, :], 0.0)
                chunk_bodies(dve, body)
                if g == 2:
                    for step in range(UC):
                        features(NC // UC - 1, NC - UC, step)

            def edges(l):
                def one_hot(k, m, u):
                    dve.wait_ge(rel_loaded[u % S], (m + u // S) * 16)
                    dve.wait_ge(es["logit_done1"], k + (u - 2))
                    TS(oh[:, u % 3, :], rel_b[:, u % S, :], const("slot", KO), None, ALU.is_equal
                       ).then_inc(es["oh_done"], 1)

                def relu_last(k, u):
                    n = ZQ[2]
                    dve.wait_ge(es["logit_done1"], k + (u - 1))
                    dve.wait_ge(es["z_done2"], k + (u + 1))
                    TS(relu[0:n, u % 2, 2, :], ps[0:n, 2, :], 0.0, None, ALU.max).then_inc(es["relu_done2"], 1)

                def maxima(k, u, hh):
                    b = u % 2
                    dve.wait_ge(es["scale_done"], k + (u - 1))
                    dve.wait_ge(es[f"logit_done{hh}"], k + (u + 1))
                    dve.tensor_reduce(neg_item[:, b, 2 * hh:2 * hh + 2],
                                      ps[0:HW, logit_bank(u, hh), 0:2 * P].rearrange(
                                          "p (j e) -> p j e", j=2), AX.X, ALU.max, negate=True
                                      ).then_inc(es[f"max_done{hh}"], 1)

                def new_max(k, u, j, wins):
                    b = u % 2
                    if j % 2 == 0:
                        dve.wait_ge(es[f"max_done{j // 2}"], k + (u + 1))
                    m = neg_item[:, b, j:j + 1]
                    state = neg_max[:, bass.ds(wins[j], 1)]
                    dve.wait_ge(es[f"state_done{(j - 1) % U}"], k + (u if j == 0 else u + 1))
                    TT(nm[:, b, j:j + 1], m, state, ALU.min)
                    i = TS(dm[:, b, j:j + 1], m, state, 0.0, ALU.subtract, ALU.min)
                    if j % 2:
                        i.then_inc(es[f"nm_done{j // 2}"], 1)
                    TT(state, m, state, ALU.min).then_inc(es[f"state_done{j}"], 1)

                def take_sum(k, u, j, wins):
                    if j == 0:
                        dve.wait_ge(es["sum_done"], k + (u + 1))
                        dve.wait_ge(es["scale_done"], k + (u + 1))
                    a = acc[:, bass.ds(wins[j], 1), :].rearrange("p a f -> p (a f)")
                    dve.wait_ge(es[f"acc_done{(j - 1) % U}"], k + (u if j == 0 else u + 1))
                    STT(a, a, scale[:, u % 2, j:j + 1], ps[0:HW, 6, j * (F + 1):(j + 1) * (F + 1)],
                        ALU.mult, ALU.add).then_inc(es[f"acc_done{j}"], 1)

                def per_round(r, k):
                    dve.wait_ge(tab_loaded[l], (r + 1) * 32)

                def body(q, k, m, is_first, is_last):
                    col = q * ITER
                    if is_first:
                        one_hot(k, m, 0)
                        one_hot(k, m, 1)
                    wins = {}
                    for u in range(S + 2 if is_last else S):
                        lag1 = not (is_first and u < 1) and u <= S
                        lag2 = not (is_first and u < 2)
                        for v in (u - 2, u - 1):
                            if v not in wins and (not is_first or v >= 0) and v < S:
                                wins[v] = window_regs(dve, mybir.EngineType.DVE, win_s, col + v * U, W)
                        if u < S:
                            relu_last(k, u)
                        if lag1:
                            maxima(k, u - 1, 0)
                            new_max(k, u - 1, 0, wins[u - 1])
                            new_max(k, u - 1, 1, wins[u - 1])
                            maxima(k, u - 1, 1)
                            new_max(k, u - 1, 2, wins[u - 1])
                        if lag2:
                            take_sum(k, u - 2, 0, wins[u - 2])
                        if lag1:
                            new_max(k, u - 1, 3, wins[u - 1])
                        if lag2:
                            take_sum(k, u - 2, 1, wins[u - 2])
                        if not (is_last and u + 2 >= S):
                            one_hot(k, m, u + 2)
                        if lag2:
                            take_sum(k, u - 2, 2, wins[u - 2])
                            take_sum(k, u - 2, 3, wins[u - 2])
                edge_rounds(dve, l, per_round, body)

            for l in range(2):
                node_stage(l)
                barrier(dve, 2 + 2 * l)
                dve.wait_ge(acc_init, 16 * H * (NC // UC) * (l + 1))
                edges(l)
                barrier(dve, 3 + 2 * l)
            node_stage(2)
            barrier(dve, 6)

            def product(k, m, u):
                dve.wait_ge(ea_loaded[u % S], (m + u // S) * (16 * U))
                dve.wait_ge(gs["pa_done"], k + (u - 1))
                e = ea[:, u % S, :, :]
                TT(e, e, ps_row[:, :].unsqueeze(1).to_broadcast([P, U, F]), ALU.mult).then_inc(gs["prod_done"], 1)
                dve.wait_ge(gs["prod_done"], k + (u + 1))
                dve.tensor_reduce(pre[:, u % 2, :], e, AX.X, ALU.add).then_inc(gs["pre_done"], 1)

            def gates(k, u, col):
                TT(oh2[:, :, :], tile_rel[:, bass.ds(col, U)].unsqueeze(2).to_broadcast([P, U, SPAN]),
                   cst[:, at["item_row"][0]:at["item_row"][0] + SPAN].unsqueeze(1).to_broadcast([P, U, SPAN]),
                   ALU.is_equal).then_inc(gs["oh2_done"], 1)
                dve.wait_ge(gs["oh2_done"], k + (u + 1))
                dve.wait_ge(gs["pa_done"], k + (u + 1))
                dve.wait_ge(gs["sum2_done"], k + (u - 1))
                TT(gate[:, u % 2, :, :], oh2[:, :, :], pa[:, u % 2, :].unsqueeze(2).to_broadcast([P, U, SPAN]),
                   ALU.mult).then_inc(gs["gate_done"], 1)

            def take_sums2(k, u, col):
                lows = window_regs(dve, mybir.EngineType.DVE, tile_lo, col, N)
                dve.wait_ge(gs["sum2_done"], k + (u + 1))
                for j in range(U):
                    a = acc2[:, bass.ds(lows[j], SPAN)]
                    dve.wait_ge(gs[f"acc2_done{(j - 1) % U}"], k + (u if j == 0 else u + 1))
                    TT(a, a, ps[0:F, u % 2, j * SPAN:(j + 1) * SPAN], ALU.add).then_inc(gs[f"acc2_done{j}"], 1)

            def body2(q, k, m, is_first, is_last):
                if is_first:
                    product(k, m, 0)
                for u in range(S):
                    if not (is_last and u == S - 1):
                        product(k, m, u + 1)
                    gates(k, u, q * ITER + u * U)
                    if not (is_first and u == 0):
                        take_sums2(k, u - 1, q * ITER + (u - 1) * U)
                if is_last:
                    take_sums2(k, S - 1, q * ITER + (S - 1) * U)
                    settle()
                    TS(tile_rel[:, :], tile_rel[:, :], -float(SPAN), None, ALU.add)
                    CP(lo_f[:, :], tile_lo[:, :])
                    settle()
                    TS(lo_f[:, :], lo_f[:, :], float(SPAN), float(N), ALU.add, ALU.min)
                    settle()
                    CP(tile_lo[:, :], lo_f[:, :])
                    settle()
            edge_rounds(dve, 2, lambda r, k: None, body2)
            settle()
            dve.memset(fl_r[:, :], 0.0).then_inc(sums_taken, 1)
            dve.wait_ge(sums_turned, 1)
            for c in range(0, NC, 8):
                n = min(8, NC - c)
                TT(xc[:, c:c + n, :], ps[0:CN, c // 8, 0:n * F].rearrange("p (c f) -> p c f", f=F),
                   ci[:, c:c + n].unsqueeze(2).to_broadcast([CN, n, F]), ALU.mult)
            settle()
            TT(xs[:, :, :], xs[:, :, :], xc[:, :, :], ALU.add).then_inc(final_done, 1)


INPUTS = ["x", "src", "dst", "edge_attr_64", "node_vec1", "node_vec1_n2",
          "L0_gnn_W1l", "L0_gnn_b1l", "L0_gnn_W1r", "L0_gnn_b1r", "L0_gnn_att1", "L0_gnn_bias1",
          "L0_gnn_W2l", "L0_gnn_b2l", "L0_gnn_W2r", "L0_gnn_b2r", "L0_gnn_att2", "L0_gnn_bias2",
          "L0_gnn_Wfc", "L0_gnn_bfc", "L1_gnn_ps_w"]


def kernel(**inputs):
    import concourse.bacc as bacc
    from concourse.bass_utils import run_bass_kernel_spmd

    nc = bacc.Bacc("TRN2", target_bir_lowering=False, num_devices=1)
    arrays, args = {}, []
    for name in INPUTS + ["constants"]:
        a = shape_constants() if name == "constants" else np.ascontiguousarray(inputs[name])
        arrays[f"in_{name}"] = a
        args.append(nc.dram_tensor(f"in_{name}", a.shape, mybir.dt.from_np(a.dtype), kind="ExternalInput").ap())
    out = nc.dram_tensor("out_0", (N, F), F32, kind="ExternalOutput").ap()
    build_program(nc, *args, out)
    result = run_bass_kernel_spmd(nc, [arrays], core_ids=[0])
    return result.results[0]["out_0"]
```
